# Optimizing a Trainium2 kernel written in Bass

```python
import numpy as np
import jax
import jax.numpy as jnp

def _softmax(x, axis=-1):
    return jax.nn.softmax(x, axis=axis)

def _gelu(x):
    return jax.nn.gelu(x, approximate=True)

def _silu(x):
    return jax.nn.silu(x)

def _sigmoid(x):
    return jax.nn.sigmoid(x)

def _layernorm(x, axis=-1, eps=1e-05):
    m = jnp.mean(x, axis=axis, keepdims=True)
    v = jnp.var(x, axis=axis, keepdims=True)
    return (x - m) / jnp.sqrt(v + eps)

def _scatter_add(tgt, idx, src, axis=0):
    return tgt.at[idx].add(src)

def _segment_sum(src, seg, n):
    return jax.ops.segment_sum(src, seg, n)
kernel_name = 'mk_xattn_ffn_d1_seqx_r4_258176'

def setup_inputs(seed: int=0):
    np.random.seed(seed)
    _w = jnp.asarray

    def _rec_inputs():
        import jax
        import jax.numpy as jnp
        _rk = jax.random.key(seed)
        x = -1.394e-06 + 0.9999 * jax.random.normal(jax.random.fold_in(_rk, 1), (32, 100, 256), jnp.float32)
        _lenS = 100 - jax.random.randint(jax.random.fold_in(_rk, 7), (32,), 0, max(1, 100 // 4) + 1, jnp.int32)
        _lenS2 = 361 - jax.random.randint(jax.random.fold_in(_rk, 8), (32,), 0, max(1, 361 // 4) + 1, jnp.int32)
        _ctx_1024P = jax.random.normal(jax.random.fold_in(_rk, 11), (32, 16, 256), jnp.float32)
        _ctx_1024c = jax.random.dirichlet(jax.random.fold_in(_rk, 511), 0.3 * jnp.ones((16,), jnp.float32), (32, 361))
        _ctx_1024t = jnp.einsum('bsk,bkd->bsd', _ctx_1024c, _ctx_1024P)
        _ctx_1024t = _ctx_1024t * jax.lax.rsqrt(jnp.mean(jnp.square(_ctx_1024t)) + 1e-12) * 0.953939
        ctx_1024 = -0.000292821 + 1.00034 * (_ctx_1024t + 0.3 * jax.random.normal(jax.random.fold_in(_rk, 611), (32, 361, 256), jnp.float32))
        return (x, ctx_1024)
    x, ctx_1024 = _rec_inputs()

    def _L0_xattn_setup():
        import jax, jax.numpy as jnp
        import numpy as np
        NUM_HEADS = 16
        D_MODEL = 256
        LN_EPS = 1e-05
        key = jax.random.key(seed)
        ks = jax.random.split(key, 10)
        B, S, D = (2, 512, D_MODEL)
        s = 1.0 / np.sqrt(D)
        return {'encoded': jax.random.normal(ks[0], (B, S, D), jnp.float32), 'decoded': jax.random.normal(ks[1], (B, S, D), jnp.float32), 'Wq': jax.random.normal(ks[2], (D, D), jnp.float32) * s, 'bq': jax.random.normal(ks[3], (D,), jnp.float32) * s, 'Wk': jax.random.normal(ks[4], (D, D), jnp.float32) * s, 'bk': jax.random.normal(ks[5], (D,), jnp.float32) * s, 'Wv': jax.random.normal(ks[6], (D, D), jnp.float32) * s, 'bv': jax.random.normal(ks[7], (D,), jnp.float32) * s, 'gamma': jnp.ones((D,), jnp.float32), 'beta': jnp.zeros((D,), jnp.float32)}
    _L0_xattn_all = _L0_xattn_setup()
    _L0_xattn_in = {k: v for k, v in _L0_xattn_all.items() if k in ('Wq', 'bq', 'Wk', 'bk', 'Wv', 'bv', 'gamma', 'beta')}
    del _L0_xattn_all

    def _L0_ffn_setup():
        import jax, jax.numpy as jnp
        import numpy as np
        E = 8
        TOP_K = 2
        LN_EPS = 1e-05

        def _layernorm(x, g, b):
            mu = jnp.mean(x, axis=-1, keepdims=True)
            var = jnp.var(x, axis=-1, keepdims=True)
            return (x - mu) * jax.lax.rsqrt(var + LN_EPS) * g + b
        key = jax.random.key(seed)
        ks = jax.random.split(key, 4)
        B, T, H, HF = (4, 512, 256, 512)
        s_in = 1.0 / np.sqrt(H)
        s_hid = 1.0 / np.sqrt(HF)
        return {'x': jax.random.normal(ks[0], (B, T, H), dtype=jnp.float32), 'ln_g': jnp.ones((H,), dtype=jnp.float32), 'ln_b': jnp.zeros((H,), dtype=jnp.float32), 'rW': jax.random.normal(ks[1], (H, E), dtype=jnp.float32) * s_in, 'rb': jnp.zeros((E,), dtype=jnp.float32), 'W1': jax.random.normal(ks[2], (E, H, HF), dtype=jnp.float32) * s_in, 'b1': jnp.zeros((E, HF), dtype=jnp.float32), 'W2': jax.random.normal(ks[3], (E, HF, H), dtype=jnp.float32) * s_hid, 'b2': jnp.zeros((E, H), dtype=jnp.float32)}
    _L0_ffn_all = _L0_ffn_setup()
    _L0_ffn_in = {k: v for k, v in _L0_ffn_all.items() if k in ('ln_g', 'ln_b', 'rW', 'rb', 'W1', 'b1', 'W2', 'b2')}
    del _L0_ffn_all
    return {'x': x, 'ctx_1024': ctx_1024, 'L0_xattn_Wq': _L0_xattn_in['Wq'], 'L0_xattn_bq': _L0_xattn_in['bq'], 'L0_xattn_Wk': _L0_xattn_in['Wk'], 'L0_xattn_bk': _L0_xattn_in['bk'], 'L0_xattn_Wv': _L0_xattn_in['Wv'], 'L0_xattn_bv': _L0_xattn_in['bv'], 'L0_xattn_gamma': _L0_xattn_in['gamma'], 'L0_xattn_beta': _L0_xattn_in['beta'], 'L0_ffn_ln_g': _L0_ffn_in['ln_g'], 'L0_ffn_ln_b': _L0_ffn_in['ln_b'], 'L0_ffn_rW': _L0_ffn_in['rW'], 'L0_ffn_rb': _L0_ffn_in['rb'], 'L0_ffn_W1': _L0_ffn_in['W1'], 'L0_ffn_b1': _L0_ffn_in['b1'], 'L0_ffn_W2': _L0_ffn_in['W2'], 'L0_ffn_b2': _L0_ffn_in['b2']}

def reference(x, ctx_1024, L0_xattn_Wq, L0_xattn_bq, L0_xattn_Wk, L0_xattn_bk, L0_xattn_Wv, L0_xattn_bv, L0_xattn_gamma, L0_xattn_beta, L0_ffn_ln_g, L0_ffn_ln_b, L0_ffn_rW, L0_ffn_rb, L0_ffn_W1, L0_ffn_b1, L0_ffn_W2, L0_ffn_b2):
    import jax
    import jax.numpy as jnp

    def _L0_xattn_ref(encoded, decoded, Wq, bq, Wk, bk, Wv, bv, gamma, beta):
        import jax, jax.numpy as jnp
        import numpy as np
        NUM_HEADS = 16
        D_MODEL = 256
        LN_EPS = 1e-05
        B, Sq, D = decoded.shape
        H = NUM_HEADS
        dh = D // H
        q = decoded @ Wq.T + bq
        k = encoded @ Wk.T + bk
        v = encoded @ Wv.T + bv
        q = q.reshape(B, Sq, H, dh).transpose(0, 2, 1, 3)
        k = k.reshape(B, -1, H, dh).transpose(0, 2, 1, 3)
        v = v.reshape(B, -1, H, dh).transpose(0, 2, 1, 3)
        qk = jnp.einsum('bhqd,bhkd->bhqk', q, k)
        qk = jnp.where(jnp.isnan(qk), -jnp.inf, qk)
        attn = jax.nn.softmax(qk, axis=-1)
        attn = jnp.where(jnp.isnan(attn), 0.0, attn)
        v = jnp.where(jnp.isnan(v), 0.0, v)
        z = jnp.einsum('bhqk,bhkd->bhqd', attn, v)
        z = z.reshape(B, Sq, D)
        x = z + decoded
        mu = jnp.mean(x, axis=-1, keepdims=True)
        var = jnp.var(x, axis=-1, keepdims=True)
        return (x - mu) * jax.lax.rsqrt(var + LN_EPS) * gamma + beta

    def _L0_ffn_ref(x, ln_g, ln_b, rW, rb, W1, b1, W2, b2):
        import jax, jax.numpy as jnp
        import numpy as np
        E = 8
        TOP_K = 2
        LN_EPS = 1e-05

        def _layernorm(x, g, b):
            mu = jnp.mean(x, axis=-1, keepdims=True)
            var = jnp.var(x, axis=-1, keepdims=True)
            return (x - mu) * jax.lax.rsqrt(var + LN_EPS) * g + b
        z = _layernorm(x, ln_g, ln_b)
        logits = jnp.einsum('bth,he->bte', z, rW) + rb
        probs = jax.nn.softmax(logits, axis=-1)
        topv, topi = jax.lax.top_k(probs, TOP_K)
        mask = jnp.sum(jax.nn.one_hot(topi, E, dtype=probs.dtype) * topv[..., None], axis=-2)
        denom = jnp.maximum(jnp.sum(mask, axis=-1, keepdims=True), 1e-08)
        w = mask / denom
        hid = jax.nn.gelu(jnp.einsum('bth,ehf->btef', z, W1) + b1, approximate=False)
        outs = jnp.einsum('btef,efh->bteh', hid, W2) + b2
        mixed = jnp.sum(outs * w[..., None], axis=2)
        return x + mixed
    x = x + _L0_xattn_ref(ctx_1024, _layernorm(x, axis=-1), L0_xattn_Wq, L0_xattn_bq, L0_xattn_Wk, L0_xattn_bk, L0_xattn_Wv, L0_xattn_bv, L0_xattn_gamma, L0_xattn_beta)
    x = x + _L0_ffn_ref(_layernorm(x, axis=-1), L0_ffn_ln_g, L0_ffn_ln_b, L0_ffn_rW, L0_ffn_rb, L0_ffn_W1, L0_ffn_b1, L0_ffn_W2, L0_ffn_b2)
    return x

_drawn_inputs = setup_inputs


def setup_inputs(seed=0):
    import zlib

    import numpy as np

    out = dict(_drawn_inputs(seed))
    spreads = {'L0_xattn_gamma': (1.0, 0.2),
     'L0_xattn_beta': (0.0, 0.1),
     'L0_ffn_ln_g': (1.0, 0.2),
     'L0_ffn_ln_b': (0.0, 0.1),
     'L0_ffn_rb': (0.0, 0.1),
     'L0_ffn_b1': (0.0, 0.461),
     'L0_ffn_b2': (0.0, 0.312)}
    factors = {'L0_xattn_bk': 8.0}
    for name, (base, spread) in spreads.items():
        noise = np.random.default_rng([zlib.crc32(name.encode()), seed]).standard_normal(out[name].shape)
        drawn = base * np.exp(spread * noise) if base else spread * noise
        out[name] = jnp.asarray(drawn.astype(out[name].dtype))
    for name, factor in factors.items():
        out[name] = (out[name] * factor).astype(out[name].dtype)
    return out
```

```python
import concourse.bass as bass
from concourse import mybir
from contextlib import ExitStack

FP32 = mybir.dt.float32
BF16 = mybir.dt.bfloat16
I32 = mybir.dt.int32
ALU = mybir.AluOpType
ACT = mybir.ActivationFunctionType
AXIS = mybir.AxisListType

B, Q, D = 32, 100, 256
KEYS = 361
H, DH = 16, 16
E, HF = 8, 512
EPS = 1e-5
KT = 3
KPAD = KT * 128
LAST = KEYS - 2 * 128
PROD = [0, 0, 0, 1, 1, 2]
QPART = [0, 1, 2, 0, 1, 0]
ROWS = 16 * len(PROD)
MROWS = ROWS + 3
G = 4
NG = G * KT
TINY = 1e-30
MAGIC = 0x5F3759DF


class Batch:

    def __init__(self, turn, c):
        self.index = turn * 3 + c if c or isinstance(turn, int) else turn * 3
        self.slot = c % 3
        self.turn = turn + c // 3 if c // 3 else turn
        self.known = isinstance(turn, int)

    def valid(self):
        return not self.known or 0 <= self.index < B


def after(eng, sem, value):
    if isinstance(value, int) and value <= 0:
        return
    eng.wait_ge(sem, value)


def pipeline(eng, iteration):
    for i in range(-2, 3):
        iteration(0, i)
    with eng.Fori(1, 10) as turn:
        for r in range(3):
            iteration(turn, r)
    for i in range(30, 34):
        iteration(0, i)


def build(nc, x, ctx_t, wq_t, bq, wk_t, bk, wv_t, bv, gamma, beta, ln_g, ln_b, rw, rb, w1, b1, w2, b2,
          ident_d, kscr, qscr, zscr, out):
    es = ExitStack()
    with es:
        def sem(name):
            return es.enter_context(nc.semaphore(name))

        def sb(stack, name, shape, dt=FP32):
            return stack.enter_context(nc.sbuf_tensor(name, shape, dt))

        def pb(stack, name, shape, dt=FP32):
            return stack.enter_context(nc.psum_tensor(name, shape, dt))

        x_all = sb(es, "x_all", [Q, B, D])
        zf_all = sb(es, "zf_all", [Q, B, D])
        ident = sb(es, "ident", [128, 128])
        mean0 = sb(es, "mean0", [Q, B])
        rstd0 = sb(es, "rstd0", [Q, B])

        x_loaded = [sem(f"x_loaded{k}") for k in range(4)]
        const_loaded = sem("const_loaded")
        N_CONST = 13
        memsets = sem("memsets")
        ln0_step = sem("ln0_step")
        stats0_done = sem("stats0_done")
        out_stored = sem("out_stored")

        att = ExitStack()
        with att:
            stats0 = sb(att, "stats0", [Q, B, 6])
            ln0 = [sb(att, f"ln0_{k}", [Q, B]) for k in range(4)]
            ct = sb(att, "ct", [128, 3, 2, KPAD])
            wq_s = sb(att, "wq_s", [128, 2, D])
            wk_s = sb(att, "wk_s", [128, 2, D])
            wv_s = sb(att, "wv_s", [128, 2, D])
            bq_s = sb(att, "bq_s", [128, 2])
            bk_s = sb(att, "bk_s", [128, 2])
            bv_s = sb(att, "bv_s", [128, D])
            row_c = [sb(att, f"row_c{k}", [Q, D]) for k in range(4)]
            drow = sb(att, "drow", [Q, D])
            dt_s = sb(att, "dt_s", [128, 2, Q])
            q_part = sb(att, "q_part", [128, 3, 2, Q], BF16)
            q_rest = sb(att, "q_rest", [128, 2, Q])
            k_part = sb(att, "k_part", [128, 3, 2, KEYS], BF16)
            k_rest = sb(att, "k_rest", [128, 2, KEYS])
            k_stack = sb(att, "k_stack", [128, 3, H, KPAD], BF16)
            q_stack = sb(att, "q_stack", [128, 3, H, Q], BF16)
            v_raw = sb(att, "v_raw", [128, KT * H, DH])
            v_neg = sb(att, "v_neg", [128, KT * H, DH])
            v_aug = sb(att, "v_aug", [128, 3, KT * H, 32])
            negmax = sb(att, "negmax", [Q, H])
            m_part = sb(att, "m_part", [H, 3, Q], BF16)
            m_rest = sb(att, "m_rest", [H, Q])
            p_t = sb(att, "p_t", [128, 4, 4 * Q])
            zt_s = sb(att, "zt_s", [128, G * Q])
            den = sb(att, "den", [Q, H])
            rden = sb(att, "rden", [Q, H])
            zn = sb(att, "zn", [Q, H, DH])
            z_in = sb(att, "z_in", [Q, 3, D])
            u = sb(att, "u", [Q, D])
            y = sb(att, "y", [Q, D])
            t1 = sb(att, "t1", [Q, D])
            st6 = sb(att, "st6", [Q, 6])
            mv = sb(att, "mv", [Q, 2])
            ln_t = [sb(att, f"ln_t{k}", [Q, 1]) for k in range(4)]

            s_row = [pb(att, f"s_row{k}", [128, 512]) for k in range(2)]
            s_t = [pb(att, f"s_t{k}", [128, 512]) for k in range(2)]
            pj = [pb(att, f"pj{k}", [128, 512]) for k in range(2)]
            zt = pb(att, "zt", [128, 512])
            tr = pb(att, "tr", [128, 512])

            ctx_loaded = [sem(f"ctx_loaded{k}") for k in range(3)]
            k_stored = [sem(f"k_stored{k}") for k in range(3)]
            q_stored = [sem(f"q_stored{k}") for k in range(3)]
            k_stacked = [sem(f"k_stacked{k}") for k in range(3)]
            q_stacked = [sem(f"q_stacked{k}") for k in range(3)]
            z_stored = [sem(f"z_stored{k}") for k in range(3)]
            z_loaded = [sem(f"z_loaded{k}") for k in range(3)]
            m_stacked = [sem(f"m_stacked{k}") for k in range(3)]
            d_ready, dt_done, dt_copied = sem("d_ready"), sem("dt_done"), sem("dt_copied")
            q_done, k_done, v_done = sem("q_done"), sem("k_done"), sem("v_done")
            qh_ready, qm_ready, kh_ready, km_ready = sem("qh_ready"), sem("qm_ready"), sem("kh_ready"), sem("km_ready")
            q_rest_ready, q_low_ready = sem("q_rest_ready"), sem("q_low_ready")
            k_rest_ready, k_low_ready = sem("k_rest_ready"), sem("k_low_ready")
            v_biased, v_neg_ready, v_ready = sem("v_biased"), sem("v_neg_ready"), sem("v_ready")
            s_row_done, max_done = sem("s_row_done"), sem("max_done")
            mt_done, m_step = sem("mt_done"), sem("m_step")
            s_t_done, exp_done, p_ready, pv_done = sem("s_t_done"), sem("exp_done"), sem("p_ready"), sem("pv_done")
            zt_copied, zrow_done, z_step, tail_step = sem("zt_copied"), sem("zrow_done"), sem("z_step"), sem("tail_step")
            M_STEPS = 4
            Z_STEPS = 3

            blk = att.enter_context(nc.Block())

            @blk.sync
            def _(sp):
                sp.dma_start(ident[:], ident_d).then_inc(const_loaded, 16)
                sp.dma_start(wq_s[:], wq_t).then_inc(const_loaded, 16)
                sp.dma_start(wk_s[:], wk_t).then_inc(const_loaded, 16)
                sp.dma_start(wv_s[:], wv_t).then_inc(const_loaded, 16)
                sp.dma_start(bq_s[:], bq).then_inc(const_loaded, 16)
                sp.dma_start(bk_s[:], bk).then_inc(const_loaded, 16)
                sp.dma_start(bv_s[:], bv.unsqueeze(0).broadcast_to([128, D])).then_inc(const_loaded, 16)
                for dst, src in zip(row_c, (gamma, beta, ln_g, ln_b)):
                    sp.dma_start(dst[:], src.unsqueeze(0).broadcast_to([Q, D])).then_inc(const_loaded, 16)
                xv = x.rearrange("b q d -> q b d")
                for k in range(4):
                    sp.dma_start(x_all[:, 8 * k:8 * k + 8, :], xv[:, 8 * k:8 * k + 8, :]).then_inc(x_loaded[k], 16)

                def iteration(turn, i):
                    a, m, d = Batch(turn, i + 2), Batch(turn, i + 1), Batch(turn, i - 1)
                    if a.valid():
                        after(sp, s_t_done, NG * (a.index - 2))
                        sp.dma_start(ct[:, a.slot, :, 0:KEYS], ctx_t[a.index]).then_inc(ctx_loaded[a.slot], 16)
                    if d.valid():
                        sp.wait_ge(z_step, Z_STEPS * d.index + Z_STEPS)
                        sp.dma_start(zscr[d.slot].rearrange("h q w -> q h w"), zn[:]).then_inc(z_stored[d.slot], 16)
                    if a.valid():
                        sp.wait_ge(q_low_ready, a.index + 1)
                        for s in range(3):
                            sp.dma_start(qscr[a.slot, s], q_part[:, s]).then_inc(q_stored[a.slot], 16)
                        sp.wait_ge(k_low_ready, a.index + 1)
                        for s in range(3):
                            sp.dma_start(kscr[a.slot, s], k_part[:, s]).then_inc(k_stored[a.slot], 16)
                    if d.valid():
                        sp.wait_ge(z_stored[d.slot], 16 * d.turn + 16)
                        rows = zscr[d.slot].rearrange("h q w -> (h q w)").rearrange("(r n) -> r n", n=D)
                        sp.dma_start(z_in[:, d.slot], rows).then_inc(z_loaded[d.slot], 16)
                    if a.valid():
                        sp.wait_ge(q_stored[a.slot], 48 * a.turn + 48)
                        for g, s in enumerate(QPART):
                            src = qscr[a.slot, s].rearrange("(h d) t k -> d t h k", d=DH)
                            dst = q_stack[16 * g:16 * g + 16, a.slot].rearrange("d (t h) k -> d t h k", t=2)
                            sp.dma_start(dst, src).then_inc(q_stacked[a.slot], 16)
                        sp.wait_ge(k_stored[a.slot], 48 * a.turn + 48)
                        for g, s in enumerate(PROD):
                            src = kscr[a.slot, s].rearrange("(h d) t k -> d t h k", d=DH)
                            dst = k_stack[16 * g:16 * g + 16, a.slot, :, 0:KEYS].rearrange("d (t h) k -> d t h k", t=2)
                            sp.dma_start(dst, src).then_inc(k_stacked[a.slot], 16)
                    if m.valid():
                        sp.wait_ge(m_step, M_STEPS * m.index + M_STEPS)
                        for s in range(3):
                            sp.dma_start(q_stack[ROWS + s:ROWS + s + 1, m.slot], m_part[:, s]).then_inc(m_stacked[m.slot], 16)

                sp.wait_ge(memsets, 5)
                pipeline(sp, iteration)

            @blk.gpsimd
            def _(pool):
                for n, (dst, fill) in enumerate(((ct[:, :, :, KEYS:KPAD], 0.0), (k_stack[:, :, :, KEYS:KPAD], 0.0),
                                                 (k_stack[ROWS:128, :, :, 0:KEYS], 1.0), (v_aug[:, :, :, DH:32], 0.0),
                                                 (v_aug[:, :, :, DH:DH + 1], 1.0))):
                    nc.gpsimd.memset(dst, fill).then_inc(memsets, 1)
                    pool.wait_ge(memsets, n + 1)

            @blk.tensor
            def _(pe):
                def project(b, item):
                    if item == 0:
                        pe.wait_ge(d_ready, b.index + 1)
                        after(pe, v_biased, 2 * b.index - 1)
                        for c in range(2):
                            last = nc.tensor.transpose(pj[0][:, c * Q:c * Q + Q], drow[:, c * 128:c * 128 + 128], ident[0:Q, 0:Q])
                        last.then_inc(dt_done, 1)
                    elif item == 1:
                        pe.wait_ge(dt_copied, b.index + 1)
                        after(pe, v_biased, 2 * b.index)
                        for t in range(2):
                            for c in range(2):
                                last = nc.tensor.matmul(pj[1][:, t * Q:t * Q + Q], wq_s[:, c, t * 128:t * 128 + 128],
                                                        dt_s[:, c, :], start=(c == 0), stop=(c == 1))
                        last.then_inc(q_done, 1)
                    elif item < 4:
                        t = item - 2
                        if t == 0:
                            pe.wait_ge(ctx_loaded[b.slot], 16 * b.turn + 16)
                        else:
                            pe.wait_ge(q_rest_ready, 2 * b.index + 2)
                        for c in range(2):
                            last = nc.tensor.matmul(pj[t][:, 0:KEYS], wk_s[:, c, t * 128:t * 128 + 128],
                                                    ct[:, b.slot, c, 0:KEYS], start=(c == 0), stop=(c == 1))
                        last.then_inc(k_done, 1)
                    else:
                        n = item - 4
                        pe.wait_ge(k_rest_ready, 2 * b.index + 1 + n)
                        for kt in ((0, 1), (2,))[n]:
                            for c in range(2):
                                last = nc.tensor.matmul(pj[n][:, kt % 2 * D:kt % 2 * D + D], ct[:, b.slot, c, kt * 128:kt * 128 + 128],
                                                        wv_s[:, c, :], start=(c == 0), stop=(c == 1))
                        last.then_inc(v_done, 1)

                def score_rows(b, h):
                    if h == 0:
                        pe.wait_ge(q_stacked[b.slot], 96 * b.turn + 96)
                        pe.wait_ge(k_stacked[b.slot], 96 * b.turn + 96)
                    after(pe, max_done, H * b.index + h - 1)
                    nc.tensor.matmul(s_row[h % 2][0:Q, 0:KEYS], q_stack[0:ROWS, b.slot, h, :],
                                     k_stack[0:ROWS, b.slot, h, 0:KEYS], start=True, stop=True).then_inc(s_row_done, 1)

                def max_transposed(b):
                    pe.wait_ge(max_done, H * b.index + H)
                    after(pe, z_step, Z_STEPS * (b.index - 1))
                    nc.tensor.transpose(tr[0:H, 0:Q], negmax[:], ident[0:Q, 0:Q]).then_inc(mt_done, 1)

                def scores(b, g):
                    if g == 0:
                        pe.wait_ge(m_stacked[b.slot], 48 * b.turn + 48)
                    after(pe, exp_done, NG * b.index + g - 1)
                    for j in range(4):
                        h, kt = 4 * (g // KT) + j, g % KT
                        last = nc.tensor.matmul(s_t[g % 2][:, j * Q:j * Q + Q], k_stack[0:MROWS, b.slot, h, kt * 128:kt * 128 + 128],
                                                q_stack[0:MROWS, b.slot, h, :], start=True, stop=True)
                    last.then_inc(s_t_done, 1)

                def values(b, g):
                    if g == 0:
                        pe.wait_ge(v_ready, b.index + 1)
                        after(pe, zt_copied, b.index)
                    pe.wait_ge(p_ready, NG * b.index + g + 1)
                    kt, grp = g % KT, g // KT
                    n = LAST if kt == KT - 1 else 128
                    for j in range(4):
                        last = nc.tensor.matmul(zt[32 * j:32 * j + 32, grp * Q:grp * Q + Q], v_aug[0:n, b.slot, kt * H + 4 * grp + j, :],
                                                p_t[0:n, g % 4, j * Q:j * Q + Q], start=(kt == 0), stop=(kt == KT - 1))
                    last.then_inc(pv_done, 1)

                def z_rows(b):
                    pe.wait_ge(zt_copied, b.index + 1)
                    pe.wait_ge(m_step, M_STEPS * (b.index + 1) + M_STEPS) if not (b.known and b.index == B - 1) else None
                    for grp in range(G):
                        last = nc.tensor.transpose(tr[0:Q, grp * 128:grp * 128 + 128], zt_s[:, grp * Q:grp * Q + Q], ident[:])
                    last.then_inc(zrow_done, 1)

                pe.wait_ge(const_loaded, 16 * 11)
                pe.wait_ge(memsets, 5)

                def iteration(turn, i):
                    a, b, c, d = (Batch(turn, i + k) for k in (2, 1, 0, -1))
                    for s in range(NG + 2):
                        if c.valid() and s < NG:
                            scores(c, s)
                        if c.valid() and s >= 2:
                            values(c, s - 2)
                        if b.valid() and s < 8:
                            score_rows(b, 2 * s)
                            score_rows(b, 2 * s + 1)
                        if a.valid() and s < 6:
                            project(a, s)
                        if d.valid() and s == 2:
                            z_rows(d)
                        if b.valid() and s == 10:
                            max_transposed(b)

                pipeline(pe, iteration)

            @blk.scalar
            def _(act):
                def copy_parts(a, item):
                    if item == 0:
                        act.wait_ge(dt_done, a.index + 1)
                        after(act, q_done, a.index)
                        nc.scalar.activation(dt_s[:, :, :].rearrange("p c k -> p (c k)"), pj[0][:, 0:2 * Q], ACT.Copy).then_inc(dt_copied, 1)
                    elif item == 1:
                        act.wait_ge(q_done, a.index + 1)
                        before = Batch(a.turn if not a.known else 0, 0)
                        for t in range(2):
                            nc.scalar.activation(q_part[:, 0, t, :], pj[1][:, t * Q:t * Q + Q], ACT.Identity,
                                                 bias=bq_s[:, t:t + 1]).then_inc(qh_ready, 1)
                    elif item < 4:
                        t = item - 2
                        act.wait_ge(k_done, 2 * a.index + 1 + t)
                        nc.scalar.activation(k_part[:, 0, t, :], pj[t][:, 0:KEYS], ACT.Identity,
                                             bias=bk_s[:, t:t + 1]).then_inc(kh_ready, 1)
                    elif item == 4:
                        act.wait_ge(q_rest_ready, 2 * a.index + 2)
                        nc.scalar.activation(q_part[:, 1], q_rest[:], ACT.Copy).then_inc(qm_ready, 1)
                    elif item == 5:
                        act.wait_ge(k_rest_ready, 2 * a.index + 2)
                        nc.scalar.activation(k_part[:, 1], k_rest[:], ACT.Copy).then_inc(km_ready, 1)

                def exponentials(b, g):
                    act.wait_ge(s_t_done, NG * b.index + g + 1)
                    after(act, pv_done, NG * b.index + g - 3)
                    nc.scalar.activation(p_t[:, g % 4, :], s_t[g % 2][:, 0:4 * Q], ACT.Exp).then_inc(exp_done, 1)

                act.wait_ge(const_loaded, 16 * 11)

                def iteration(turn, i):
                    a, p, c, d = (Batch(turn, i + k) for k in (2, 1, 0, -1))
                    if d.valid():
                        act.wait_ge(pv_done, NG * d.index + NG)
                        after(act, zrow_done, d.index)
                        nc.scalar.activation(zt_s[:], zt[:, 0:G * Q], ACT.Copy).then_inc(zt_copied, 1)
                    for s in range(NG):
                        if c.valid():
                            exponentials(c, s)
                        if a.valid() and s < 6:
                            if s == 1 and p.valid():
                                act.wait_ge(q_stored[p.slot], 48 * p.turn + 48)
                                act.wait_ge(k_stored[p.slot], 48 * p.turn + 48)
                            copy_parts(a, s)

                pipeline(act, iteration)

            @blk.vector
            def _(dve):
                v = nc.vector
                dve.wait_ge(x_loaded[0], 16)
                dve.wait_ge(x_loaded[1], 16)
                dve.wait_ge(x_loaded[2], 16)
                dve.wait_ge(x_loaded[3], 16)
                dve.wait_ge(const_loaded, 16 * 11)
                with dve.Fori(0, B) as b:
                    v.bn_stats(stats0[:, b, :], x_all[:, b, :]).then_inc(stats0_done, 1)
                dve.wait_ge(stats0_done, B)
                count = [0]

                def step0(ins):
                    count[0] += 1
                    ins.then_inc(ln0_step, 1)
                    dve.wait_ge(ln0_step, count[0])

                me, mo = stats0[:, :, 1], stats0[:, :, 4]
                step0(v.tensor_tensor(ln0[0][:], me, mo, ALU.add))
                step0(v.tensor_scalar(mean0[:], ln0[0][:], 0.5, None, ALU.mult))
                step0(v.tensor_tensor(ln0[0][:], me, mo, ALU.subtract))
                step0(v.tensor_tensor(ln0[1][:], ln0[0][:], ln0[0][:], ALU.mult))
                step0(v.tensor_tensor(ln0[2][:], stats0[:, :, 2], stats0[:, :, 5], ALU.add))
                step0(v.tensor_scalar(ln0[1][:], ln0[1][:], 0.25, EPS, ALU.mult, ALU.add))
                step0(v.tensor_scalar(ln0[2][:], ln0[2][:], 1.0 / D, None, ALU.mult))
                step0(v.tensor_tensor(ln0[0][:], ln0[2][:], ln0[1][:], ALU.add))

                def rsqrt(step, out_, var, a, b_):
                    step(v.tensor_scalar(a.bitcast(I32), var.bitcast(I32), 1, None, ALU.logical_shift_right))
                    step(v.tensor_scalar(out_.bitcast(I32), a.bitcast(I32), -1.0, float(MAGIC), ALU.mult, ALU.add))
                    for _ in range(4):
                        step(v.tensor_tensor(a, out_, out_, ALU.mult))
                        step(v.tensor_tensor(a, a, var, ALU.mult))
                        step(v.tensor_scalar(b_, a, -0.5, 1.5, ALU.mult, ALU.add))
                        step(v.tensor_tensor(out_, out_, b_, ALU.mult))

                rsqrt(step0, rstd0[:], ln0[0][:], ln0[1][:], ln0[2][:])

                def projections(a, item):
                    if item == 0:
                        after(dve, dt_done, a.index)
                        v.tensor_scalar(drow[:], x_all[:, a.index, :], mean0[:, bass.ds(a.index, 1)], rstd0[:, bass.ds(a.index, 1)],
                                        ALU.subtract, ALU.mult).then_inc(d_ready, 1)
                    elif item == 1:
                        for t in range(2):
                            dve.wait_ge(qh_ready, 2 * a.index + 2)
                            after(dve, q_low_ready, a.index)
                            v.scalar_tensor_tensor(q_rest[:, t], pj[1][:, t * Q:t * Q + Q], bq_s[:, t:t + 1], q_part[:, 0, t, :],
                                                   ALU.add, ALU.subtract).then_inc(q_rest_ready, 1)
                    elif item < 4:
                        t = item - 2
                        dve.wait_ge(kh_ready, 2 * a.index + 1 + t)
                        after(dve, k_low_ready, a.index)
                        v.scalar_tensor_tensor(k_rest[:, t], pj[t][:, 0:KEYS], bk_s[:, t:t + 1], k_part[:, 0, t, :],
                                               ALU.add, ALU.subtract).then_inc(k_rest_ready, 1)
                    elif item == 4:
                        dve.wait_ge(v_done, 2 * a.index + 1)
                        after(dve, v_ready, a.index)
                        bias2 = bv_s[:, :].unsqueeze(1).broadcast_to([128, 2, D])
                        v.tensor_tensor(v_raw[:, 0:2 * H, :].rearrange("p (t h) d -> p t (h d)", t=2), pj[0][:, :].rearrange("p (t n) -> p t n", t=2),
                                        bias2, ALU.add).then_inc(v_biased, 1)
                        dve.wait_ge(qm_ready, a.index + 1)
                        v.tensor_tensor(q_part[:, 2], q_rest[:], q_part[:, 1], ALU.subtract).then_inc(q_low_ready, 1)
                    elif item == 5:
                        dve.wait_ge(v_done, 2 * a.index + 2)
                        v.tensor_tensor(v_raw[:, 2 * H:3 * H, :].rearrange("p h d -> p (h d)"), pj[1][:, 0:D],
                                        bv_s[:, :], ALU.add).then_inc(v_biased, 1)
                        dve.wait_ge(km_ready, a.index + 1)
                        v.tensor_tensor(k_part[:, 2], k_rest[:], k_part[:, 1], ALU.subtract).then_inc(k_low_ready, 1)
                    elif item == 6:
                        dve.wait_ge(v_biased, 2 * a.index + 2)
                        v.tensor_scalar(v_neg[:], v_raw[:], 0.0, None, ALU.min).then_inc(v_neg_ready, 1)
                    elif item == 7:
                        dve.wait_ge(v_neg_ready, a.index + 1)
                        after(dve, pv_done, NG * (a.index - 2))
                        v.scalar_tensor_tensor(v_aug[:, a.slot, :, 0:DH], v_raw[:], 0.0, v_neg[:],
                                               ALU.max, ALU.add).then_inc(v_ready, 1)

                def row_max(b, h):
                    dve.wait_ge(s_row_done, H * b.index + h + 1)
                    if h == 0:
                        after(dve, mt_done, b.index)
                    v.tensor_reduce(negmax[:, h:h + 1], s_row[h % 2][0:Q, 0:KEYS], AXIS.X, ALU.max, negate=True).then_inc(max_done, 1)

                def max_parts(b):
                    n = M_STEPS * b.index
                    dve.wait_ge(mt_done, b.index + 1)
                    p = Batch(b.turn, b.slot - 1) if not b.known else Batch(0, b.index - 1)
                    if p.valid():
                        dve.wait_ge(m_stacked[p.slot], 48 * p.turn + 48)
                    v.tensor_copy(m_part[:, 0], tr[0:H, 0:Q]).then_inc(m_step, 1)
                    dve.wait_ge(m_step, n + 1)
                    v.tensor_tensor(m_rest[:], tr[0:H, 0:Q], m_part[:, 0], ALU.subtract).then_inc(m_step, 1)
                    dve.wait_ge(m_step, n + 2)
                    v.tensor_copy(m_part[:, 1], m_rest[:]).then_inc(m_step, 1)
                    dve.wait_ge(m_step, n + 3)
                    v.tensor_tensor(m_part[:, 2], m_rest[:], m_part[:, 1], ALU.subtract).then_inc(m_step, 1)

                def guard(b, g):
                    dve.wait_ge(exp_done, NG * b.index + g + 1)
                    v.tensor_scalar(p_t[:, g % 4, :], p_t[:, g % 4, :], 0.0, None, ALU.max).then_inc(p_ready, 1)

                def z_normalised(b):
                    heads = tr[0:Q, :].rearrange("q (h w) -> q h w", w=32)
                    n = Z_STEPS * b.index
                    dve.wait_ge(zrow_done, b.index + 1)
                    v.tensor_scalar(den[:], heads[:, :, DH], TINY, None, ALU.max).then_inc(z_step, 1)
                    dve.wait_ge(z_step, n + 1)
                    v.reciprocal(rden[:], den[:]).then_inc(z_step, 1)
                    dve.wait_ge(z_step, n + 2)
                    p = Batch(b.turn, b.slot - 1) if not b.known else Batch(0, b.index - 1)
                    if p.valid():
                        dve.wait_ge(z_stored[p.slot], 16 * p.turn + 16)
                    v.tensor_tensor(zn[:], heads[:, :, 0:DH], rden[:].unsqueeze(2).broadcast_to([Q, H, DH]),
                                    ALU.mult).then_inc(z_step, 1)

                def tail(b):
                    n = [0]

                    def step(ins):
                        n[0] += 1
                        ins.then_inc(tail_step, 1)
                        dve.wait_ge(tail_step, TAIL * b.index + n[0])

                    xb = x_all[:, b.index, :]
                    step(v.tensor_scalar(t1[:], xb, mean0[:, bass.ds(b.index, 1)], rstd0[:, bass.ds(b.index, 1)],
                                         ALU.subtract, ALU.mult))
                    dve.wait_ge(z_loaded[b.slot], 16 * b.turn + 16)
                    step(v.tensor_tensor(u[:], z_in[:, b.slot, :], t1[:], ALU.add))

                    def norm(dst, src):
                        step(v.bn_stats(st6[:], src))
                        v.tensor_scalar(ln_t[2][:], st6[:, 1:2], 0.0, None, ALU.add)
                        step(v.bn_aggr(mv[:], st6[:]))
                        step(v.tensor_scalar(ln_t[0][:], mv[:, 1:2], EPS, None, ALU.add))
                        rsqrt(step, ln_t[3][:], ln_t[0][:], ln_t[1][:], ln_t[2][:])
                        step(v.tensor_scalar(dst, src, mv[:, 0:1], ln_t[3][:], ALU.subtract, ALU.mult))

                    norm(y[:], u[:])
                    step(v.tensor_tensor(y[:], y[:], row_c[0][:], ALU.mult))
                    step(v.tensor_tensor(y[:], y[:], row_c[1][:], ALU.add))
                    step(v.tensor_tensor(y[:], y[:], xb, ALU.add))
                    norm(u[:], y[:])
                    step(v.tensor_tensor(xb, y[:], u[:], ALU.add))
                    norm(t1[:], u[:])
                    step(v.tensor_tensor(t1[:], t1[:], row_c[2][:], ALU.mult))
                    step(v.tensor_tensor(zf_all[:, b.index, :], t1[:], row_c[3][:], ALU.add))
                    assert n[0] == TAIL

                def iteration(turn, i):
                    a, b, c, d, e = (Batch(turn, i + k) for k in (2, 1, 0, -1, -2))
                    for s in range(NG):
                        if a.valid() and s == 0:
                            projections(a, 0)
                        if c.valid():
                            guard(c, s)
                        if b.valid() and s < 8:
                            row_max(b, 2 * s)
                            row_max(b, 2 * s + 1)
                        if a.valid() and 1 <= s < 8:
                            projections(a, s)
                        if b.valid() and s == 10:
                            max_parts(b)
                        if d.valid() and s == 3:
                            z_normalised(d)
                        if e.valid() and s == 9:
                            tail(e)

                pipeline(dve, iteration)

        ffn = ExitStack()
        with ffn:
            w1_s = sb(ffn, "w1_s", [128, 2, E, HF])
            w2_s = sb(ffn, "w2_s", [128, 4, E, D])
            b1_s = sb(ffn, "b1_s", [Q, E, HF])
            b2_s = sb(ffn, "b2_s", [Q, E, D])
            rw_s = sb(ffn, "rw_s", [128, 2, E])
            rb_s = sb(ffn, "rb_s", [Q, E])
            zf = sb(ffn, "zf", [Q, D])
            zft = sb(ffn, "zft", [128, 2, Q])
            hid = sb(ffn, "hid", [Q, 2, HF])
            hidt = sb(ffn, "hidt", [128, 2, 4 * Q])
            yb = sb(ffn, "yb", [Q, D])
            lg = [sb(ffn, f"lg{k}", [Q, E]) for k in range(6)]
            sc = sb(ffn, "sc", [Q, 4])
            idx = sb(ffn, "idx", [Q, 8], mybir.dt.uint32)
            idf = sb(ffn, "idf", [Q, 8])
            iota8 = sb(ffn, "iota8", [Q, E])
            iota_i = sb(ffn, "iota_i", [Q, E], I32)

            p_zt = pb(ffn, "p_zt", [128, 512])
            p_h = [pb(ffn, f"p_h{k}", [128, 512]) for k in range(2)]
            p_ht = pb(ffn, "p_ht", [128, 512])
            p_y = pb(ffn, "p_y", [128, 512])
            p_l = pb(ffn, "p_l", [128, 512])

            w_loaded = sem("w_loaded")
            io = sem("io")
            zf_copied, zft_done, zft_copied, lg_done = sem("zf_copied"), sem("zft_done"), sem("zft_copied"), sem("lg_done")
            up_done, biased, gelu_done, ht_done, ht_copied, down_done = (sem(k) for k in ("up_done", "biased", "gelu_done", "ht_done", "ht_copied", "down_done"))
            rt_step, rt_exp, mix_step = sem("rt_step"), sem("rt_exp"), sem("mix_step")
            MIX = 3 * E

            blk = ffn.enter_context(nc.Block())

            @blk.sync
            def _(sp):
                for dst, src in ((rw_s, rw.rearrange("(c p) e -> p c e", p=128)), (rb_s, rb.unsqueeze(0).broadcast_to([Q, E]))):
                    sp.dma_start(dst[:], src).then_inc(w_loaded, 16)
                for e in range(E):
                    sp.dma_start(w1_s[:, :, e, :], w1[e].rearrange("(c p) f -> p c f", p=128)).then_inc(w_loaded, 16)
                    sp.dma_start(w2_s[:, :, e, :], w2[e].rearrange("(c p) f -> p c f", p=128)).then_inc(w_loaded, 16)
                sp.dma_start(b1_s[:], b1.unsqueeze(0).broadcast_to([Q, E, HF])).then_inc(w_loaded, 16)
                sp.dma_start(b2_s[:], b2.unsqueeze(0).broadcast_to([Q, E, D])).then_inc(w_loaded, 16)
                sp.wait_ge(mix_step, MIX * B)
                sp.dma_start(out.rearrange("b q d -> q b d"), x_all[:]).then_inc(out_stored, 16)
                sp.wait_ge(out_stored, 16)

            N_W = 16 * (4 + 2 * E)

            @blk.gpsimd
            def _(pool):
                nc.gpsimd.iota(iota_i[:], [[1, E]], base=0, channel_multiplier=0).then_inc(io, 1)
                pool.wait_ge(io, 1)
                nc.gpsimd.tensor_copy(iota8[:], iota_i[:]).then_inc(io, 1)

            @blk.tensor
            def _(pe):
                pe.wait_ge(w_loaded, N_W)
                with pe.Fori(0, B) as t:
                    pe.wait_ge(zf_copied, t + 1)
                    for c in range(2):
                        last = nc.tensor.transpose(p_zt[:, c * Q:c * Q + Q], zf[:, c * 128:c * 128 + 128], ident[0:Q, 0:Q])
                    last.then_inc(zft_done, 1)
                    pe.wait_ge(zft_copied, t + 1)
                    for c in range(2):
                        last = nc.tensor.matmul(p_l[0:Q, 0:E], zft[:, c, :], rw_s[:, c, :], start=(c == 0), stop=(c == 1))
                    last.then_inc(lg_done, 1)

                    def up(e):
                        if e >= 2:
                            pe.wait_ge(biased, t * E + e - 1)
                        for c in range(2):
                            last = nc.tensor.matmul(p_h[e % 2][0:Q, :], zft[:, c, :], w1_s[:, c, e, :], start=(c == 0), stop=(c == 1))
                        last.then_inc(up_done, 1)

                    up(0)
                    for e in range(E):
                        if e + 1 < E:
                            up(e + 1)
                        pe.wait_ge(gelu_done, t * E + e + 1)
                        if e:
                            pe.wait_ge(ht_copied, t * E + e)
                        for k in range(4):
                            last = nc.tensor.transpose(p_ht[:, k * Q:k * Q + Q], hid[:, e % 2, k * 128:k * 128 + 128], ident[0:Q, 0:Q])
                        last.then_inc(ht_done, 1)
                        pe.wait_ge(ht_copied, t * E + e + 1)
                        if e:
                            pe.wait_ge(mix_step, t * MIX + 3 * (e - 1) + 1)
                        for k in range(4):
                            last = nc.tensor.matmul(p_y[0:Q, 0:D], hidt[:, e % 2, k * Q:k * Q + Q], w2_s[:, k, e, :], start=(k == 0), stop=(k == 3))
                        last.then_inc(down_done, 1)

            @blk.scalar
            def _(act):
                with act.Fori(0, B) as t:
                    act.wait_ge(zft_done, t + 1)
                    nc.scalar.activation(zft[:].rearrange("p c k -> p (c k)"), p_zt[:, 0:2 * Q], ACT.Copy).then_inc(zft_copied, 1)
                    act.wait_ge(rt_step, RT * t + 3)
                    nc.scalar.activation(lg[1][:], lg[0][:], ACT.Exp, bias=sc[:, 0:1]).then_inc(rt_exp, 1)
                    for e in range(E):
                        act.wait_ge(biased, t * E + e + 1)
                        nc.scalar.activation(hid[:, e % 2, :], hid[:, e % 2, :], ACT.Gelu).then_inc(gelu_done, 1)
                        act.wait_ge(ht_done, t * E + e + 1)
                        nc.scalar.activation(hidt[:, e % 2, :], p_ht[:, 0:4 * Q], ACT.Copy).then_inc(ht_copied, 1)

            @blk.vector
            def _(dve):
                v = nc.vector
                dve.wait_ge(w_loaded, N_W)
                dve.wait_ge(io, 2)
                with dve.Fori(0, B) as t:
                    n = [0]

                    def step(ins):
                        n[0] += 1
                        ins.then_inc(rt_step, 1)
                        dve.wait_ge(rt_step, RT * t + n[0])

                    v.tensor_copy(zf[:], zf_all[:, t, :]).then_inc(zf_copied, 1)
                    dve.wait_ge(lg_done, t + 1)
                    step(v.tensor_tensor(lg[0][:], p_l[0:Q, 0:E], rb_s[:], ALU.add))
                    step(v.tensor_reduce(sc[:, 0:1], lg[0][:], AXIS.X, ALU.max, negate=True))
                    step(v.tensor_copy(sc[:, 3:4], sc[:, 0:1]))
                    dve.wait_ge(rt_exp, t + 1)
                    step(v.tensor_reduce(sc[:, 1:2], lg[1][:], AXIS.X, ALU.add))
                    step(v.reciprocal(sc[:, 2:3], sc[:, 1:2]))
                    step(v.tensor_scalar(lg[1][:], lg[1][:], sc[:, 2:3], None, ALU.mult))
                    v.tensor_copy(sc[:, 3:4], sc[:, 2:3])
                    step(v.max(lg[2][:], lg[1][:]))
                    v.tensor_copy(sc[:, 3:4], sc[:, 2:3])
                    step(v.max_index(idx[:], lg[2][:], lg[1][:]))
                    step(v.tensor_copy(idf[:], idx[:]))
                    step(v.tensor_tensor(sc[:, 1:2], lg[2][:, 0:1], lg[2][:, 1:2], ALU.add))
                    step(v.tensor_scalar(sc[:, 1:2], sc[:, 1:2], 1e-8, None, ALU.max))
                    step(v.reciprocal(sc[:, 2:3], sc[:, 1:2]))
                    step(v.tensor_scalar(lg[3][:], iota8[:], idf[:, 0:1], lg[2][:, 0:1], ALU.is_equal, ALU.mult))
                    step(v.tensor_scalar(lg[4][:], iota8[:], idf[:, 1:2], lg[2][:, 1:2], ALU.is_equal, ALU.mult))
                    step(v.tensor_tensor(lg[3][:], lg[3][:], lg[4][:], ALU.add))
                    step(v.tensor_scalar(lg[5][:], lg[3][:], sc[:, 2:3], None, ALU.mult))
                    assert n[0] == RT

                    def bias(e):
                        dve.wait_ge(up_done, t * E + e + 1)
                        if e >= 2:
                            dve.wait_ge(ht_done, t * E + e - 1)
                        v.tensor_tensor(hid[:, e % 2, :], p_h[e % 2][0:Q, :], b1_s[:, e, :], ALU.add).then_inc(biased, 1)

                    bias(0)
                    for e in range(E):
                        if e + 1 < E:
                            bias(e + 1)
                        dve.wait_ge(down_done, t * E + e + 1)
                        m = t * MIX + 3 * e
                        v.tensor_tensor(yb[:], p_y[0:Q, 0:D], b2_s[:, e, :], ALU.add).then_inc(mix_step, 1)
                        dve.wait_ge(mix_step, m + 1)
                        v.tensor_scalar(yb[:], yb[:], lg[5][:, e:e + 1], None, ALU.mult).then_inc(mix_step, 1)
                        dve.wait_ge(mix_step, m + 2)
                        v.tensor_tensor(x_all[:, t, :], x_all[:, t, :], yb[:], ALU.add).then_inc(mix_step, 1)
                        dve.wait_ge(mix_step, m + 3)


TAIL = 2 + 3 * (4 + 2 + 16) + 3 + 1 + 2
RT = 16


def kernel(**inputs):
    import numpy as np
    import concourse.bacc as bacc
    from concourse.bass_utils import run_bass_kernel_spmd

    def lay(w):
        return np.ascontiguousarray(np.asarray(w).T.reshape(2, 128, D).transpose(1, 0, 2))

    p = {k.replace("L0_", ""): np.asarray(v) for k, v in inputs.items()}
    ctx = p["ctx_1024"]
    arrays = {
        "x": p["x"],
        "ctx_t": np.ascontiguousarray(ctx.transpose(0, 2, 1).reshape(B, 2, 128, KEYS).transpose(0, 2, 1, 3)),
        "wq_t": lay(p["xattn_Wq"]), "bq": p["xattn_bq"].reshape(2, 128).T,
        "wk_t": lay(p["xattn_Wk"]), "bk": p["xattn_bk"].reshape(2, 128).T,
        "wv_t": lay(p["xattn_Wv"]), "bv": p["xattn_bv"],
        "gamma": p["xattn_gamma"], "beta": p["xattn_beta"],
        "ln_g": p["ffn_ln_g"], "ln_b": p["ffn_ln_b"], "rw": p["ffn_rW"], "rb": p["ffn_rb"],
        "w1": p["ffn_W1"], "b1": p["ffn_b1"], "w2": p["ffn_W2"], "b2": p["ffn_b2"],
        "ident_d": np.eye(128, dtype=np.float32),
    }
    nc = bacc.Bacc("TRN2", target_bir_lowering=False, num_devices=1)
    args = {k: nc.dram_tensor("in_" + k, a.shape, mybir.dt.from_np(a.dtype), kind="ExternalInput").ap() for k, a in arrays.items()}
    args["kscr"] = nc.dram_tensor("kscr", [3, 3, 128, 2, KEYS], BF16, kind="Internal").ap()
    args["qscr"] = nc.dram_tensor("qscr", [3, 3, 128, 2, Q], BF16, kind="Internal").ap()
    args["zscr"] = nc.dram_tensor("zscr", [3, H, Q, DH], FP32, kind="Internal").ap()
    args["out"] = nc.dram_tensor("out_x", [B, Q, D], FP32, kind="ExternalOutput").ap()
    build(nc, **args)
    r = run_bass_kernel_spmd(nc, [{"in_" + k: np.ascontiguousarray(a) for k, a in arrays.items()}], core_ids=[0])
    return r.results[0]["out_x"]
```

```python
import concourse.bass as bass
from concourse import mybir
from contextlib import ExitStack

FP32 = mybir.dt.float32
BF16 = mybir.dt.bfloat16
I32 = mybir.dt.int32
U32 = mybir.dt.uint32
ALU = mybir.AluOpType
ACT = mybir.ActivationFunctionType
AXIS = mybir.AxisListType

B, Q, D = 32, 100, 256
KEYS = 361
H, DH = 16, 16
E, HF = 8, 512
EPS = 1e-5
KT = 3
KPAD = KT * 128
LAST = KEYS - 2 * 128
PROD = [0, 0, 0, 1, 1, 2]
QPART = [0, 1, 2, 0, 1, 0]
ROWS = 16 * len(PROD)
MROWS = ROWS + 3
G = 4
NG = G * KT
TINY = 1e-30
MAGIC = 0x5F3759DF
NT = (2 * B * Q + E * 127) // 128
CH = 16


class Batch:

    def __init__(self, turn, c):
        self.index = turn * 3 + c if c or isinstance(turn, int) else turn * 3
        self.slot = c % 3
        self.turn = turn + c // 3 if c // 3 else turn
        self.known = isinstance(turn, int)

    def valid(self):
        return not self.known or 0 <= self.index < B


class Tile:

    def __init__(self, turn, c):
        self.known = isinstance(turn, int)
        self.base, self.c = turn, c
        self.index = turn * 2 + c if c or self.known else turn * 2
        self.slot = c % 2
        self.turn = turn + c // 2 if c // 2 else turn

    def next(self):
        return Tile(self.base, self.c + 1)


def after(eng, sem, value):
    if isinstance(value, int) and value <= 0:
        return
    eng.wait_ge(sem, value)


def pipeline(eng, iteration, first=1):
    for i in range(-2, 3 * first):
        iteration(0, i)
    with eng.Fori(first, 10) as turn:
        for r in range(3):
            iteration(turn, r)
    for i in range(30, 35):
        iteration(0, i)


def build(nc, x, ctx_t, wq_t, bq, wk_t, bk, wv_t, bv, gamma, beta, ln_g, ln_b, rw, rb, w1, b1, w2, b2,
          ident_d, route_c, sum_c, kscr, qscr, zscr, zf_d, y_d, out):
    es = ExitStack()
    with es:
        def sem(name):
            return es.enter_context(nc.semaphore(name))

        def sb(stack, name, shape, dt=FP32):
            return stack.enter_context(nc.sbuf_tensor(name, shape, dt))

        def pb(stack, name, shape, dt=FP32):
            return stack.enter_context(nc.psum_tensor(name, shape, dt))

        x_all = sb(es, "x_all", [Q, B, D])
        logits = sb(es, "logits", [Q, B, E])
        rw_s = sb(es, "rw_s", [128, 2, E])
        rb_s = sb(es, "rb_s", [Q, E])
        w1_s = sb(es, "w1_s", [128, 2, E, HF])
        ident = sb(es, "ident", [128, 128])
        mean0 = sb(es, "mean0", [Q, B])
        rstd0 = sb(es, "rstd0", [Q, B])

        x_loaded = [sem(f"x_loaded{k}") for k in range(4)]
        const_loaded = sem("const_loaded")
        N_CONST = 13
        w1_loaded = sem("w1_loaded")
        x2_step = sem("x2_step")
        memsets = sem("memsets")
        ln0_step = sem("ln0_step")
        stats0_done = sem("stats0_done")
        out_stored = sem("out_stored")

        att = ExitStack()
        with att:
            stats0 = sb(att, "stats0", [Q, B, 6])
            ln0 = [sb(att, f"ln0_{k}", [Q, B]) for k in range(4)]
            ct = sb(att, "ct", [128, 3, 2, KPAD])
            wq_s = sb(att, "wq_s", [128, 2, D])
            wk_s = sb(att, "wk_s", [128, 2, D])
            wv_s = sb(att, "wv_s", [128, 2, D])
            bq_s = sb(att, "bq_s", [128, 2])
            bk_s = sb(att, "bk_s", [128, 2])
            bv_s = sb(att, "bv_s", [128, D])
            row_c = [sb(att, f"row_c{k}", [Q, D]) for k in range(4)]
            drow = sb(att, "drow", [Q, D])
            dt_s = sb(att, "dt_s", [128, 2, Q])
            q_part = sb(att, "q_part", [128, 3, 2, Q], BF16)
            q_rest = sb(att, "q_rest", [128, 2, Q])
            k_part = sb(att, "k_part", [128, 3, 2, KEYS], BF16)
            k_rest = sb(att, "k_rest", [128, 2, KEYS])
            k_stack = sb(att, "k_stack", [128, 3, H, KPAD], BF16)
            q_stack = sb(att, "q_stack", [128, 3, H, Q], BF16)
            v_raw = sb(att, "v_raw", [128, KT * H, DH])
            v_neg = sb(att, "v_neg", [128, KT * H, DH])
            v_aug = sb(att, "v_aug", [128, 3, KT * H, 32])
            negmax = sb(att, "negmax", [Q, H])
            m_part = sb(att, "m_part", [H, 3, Q], BF16)
            m_rest = sb(att, "m_rest", [H, Q])
            p_t = sb(att, "p_t", [128, 4, 4 * Q])
            zt_s = sb(att, "zt_s", [128, G * Q])
            den = sb(att, "den", [Q, H])
            rden = sb(att, "rden", [Q, H])
            zn = sb(att, "zn", [Q, H, DH])
            z_in = sb(att, "z_in", [Q, 3, D])
            u = sb(att, "u", [Q, D])
            y = sb(att, "y", [Q, D])
            t1 = sb(att, "t1", [Q, D])
            st6 = sb(att, "st6", [Q, 6])
            mv = sb(att, "mv", [Q, 2])
            var = sb(att, "var", [Q, 1])
            rstd = sb(att, "rstd", [Q, 1])
            half = sb(att, "half", [Q, 1])
            zf_s = sb(att, "zf_s", [Q, 3, D])
            zft = sb(att, "zft", [128, 2 * Q])

            s_row = [pb(att, f"s_row{k}", [128, 512]) for k in range(2)]
            s_t = [pb(att, f"s_t{k}", [128, 512]) for k in range(2)]
            pj = [pb(att, f"pj{k}", [128, 512]) for k in range(2)]
            zt = pb(att, "zt", [128, 512])
            tr = pb(att, "tr", [128, 512])

            ctx_loaded = [sem(f"ctx_loaded{k}") for k in range(3)]
            k_stored = [sem(f"k_stored{k}") for k in range(3)]
            q_stored = [sem(f"q_stored{k}") for k in range(3)]
            k_stacked = [sem(f"k_stacked{k}") for k in range(3)]
            q_stacked = [sem(f"q_stacked{k}") for k in range(3)]
            z_stored = [sem(f"z_stored{k}") for k in range(3)]
            z_loaded = [sem(f"z_loaded{k}") for k in range(3)]
            m_stacked = [sem(f"m_stacked{k}") for k in range(3)]
            d_ready, dt_done, dt_copied = sem("d_ready"), sem("dt_done"), sem("dt_copied")
            q_done, k_done, v_done = sem("q_done"), sem("k_done"), sem("v_done")
            qh_ready, qm_ready, kh_ready, km_ready = sem("qh_ready"), sem("qm_ready"), sem("kh_ready"), sem("km_ready")
            q_rest_ready, q_low_ready = sem("q_rest_ready"), sem("q_low_ready")
            k_rest_ready, k_low_ready = sem("k_rest_ready"), sem("k_low_ready")
            v_biased, v_neg_ready, v_ready = sem("v_biased"), sem("v_neg_ready"), sem("v_ready")
            s_row_done, max_done = sem("s_row_done"), sem("max_done")
            mt_done, m_step = sem("mt_done"), sem("m_step")
            s_t_done, exp_done, p_ready, pv_done = sem("s_t_done"), sem("exp_done"), sem("p_ready"), sem("pv_done")
            zt_copied, zrow_done, z_step, tail_step = sem("zt_copied"), sem("zrow_done"), sem("z_step"), sem("tail_step")
            zf_stored = [sem(f"zf_stored{k}") for k in range(3)]
            norm_ready, rstd_ready, pool_step, zf_ready = sem("norm_ready"), sem("rstd_ready"), sem("pool_step"), sem("zf_ready")
            norm_ready_y, norm_ready_t = sem("norm_ready_y"), sem("norm_ready_t")
            POOL_STEPS = 3
            zft_done, zft_copied, logits_done, logits_ready = sem("zft_done"), sem("zft_copied"), sem("logits_done"), sem("logits_ready")
            M_STEPS = 4
            Z_STEPS = 3

            blk = att.enter_context(nc.Block())

            @blk.sync
            def _(sp):
                sp.dma_start(ident[:], ident_d).then_inc(const_loaded, 16)
                sp.dma_start(wq_s[:], wq_t).then_inc(const_loaded, 16)
                sp.dma_start(wk_s[:], wk_t).then_inc(const_loaded, 16)
                sp.dma_start(wv_s[:], wv_t).then_inc(const_loaded, 16)
                sp.dma_start(bq_s[:], bq).then_inc(const_loaded, 16)
                sp.dma_start(bk_s[:], bk).then_inc(const_loaded, 16)
                sp.dma_start(bv_s[:], bv.unsqueeze(0).broadcast_to([128, D])).then_inc(const_loaded, 16)
                for dst, src in zip(row_c, (gamma, beta, ln_g, ln_b)):
                    sp.dma_start(dst[:], src.unsqueeze(0).broadcast_to([Q, D])).then_inc(const_loaded, 16)
                sp.dma_start(rw_s[:], rw.rearrange("(c p) e -> p c e", p=128)).then_inc(const_loaded, 16)
                sp.dma_start(rb_s[:], rb.unsqueeze(0).broadcast_to([Q, E])).then_inc(const_loaded, 16)
                xv = x.rearrange("b q d -> q b d")
                for k in range(4):
                    sp.dma_start(x_all[:, 8 * k:8 * k + 8, :], xv[:, 8 * k:8 * k + 8, :]).then_inc(x_loaded[k], 16)

                def iteration(turn, i):
                    a, m, d, f = (Batch(turn, i + k) for k in (2, 1, -1, -3))
                    if f.valid():
                        sp.wait_ge(zf_ready, f.index + 1)
                        sp.dma_start(zf_d[f.index], zf_s[:, f.slot]).then_inc(zf_stored[f.slot], 16)
                    if a.valid():
                        after(sp, s_t_done, NG * (a.index - 2))
                        sp.dma_start(ct[:, a.slot, :, 0:KEYS], ctx_t[a.index]).then_inc(ctx_loaded[a.slot], 16)
                    if d.valid():
                        sp.wait_ge(z_step, Z_STEPS * d.index + Z_STEPS)
                        sp.dma_start(zscr[d.slot].rearrange("h q w -> q h w"), zn[:]).then_inc(z_stored[d.slot], 16)
                    if a.valid():
                        sp.wait_ge(q_low_ready, a.index + 1)
                        for s in range(3):
                            sp.dma_start(qscr[a.slot, s], q_part[:, s]).then_inc(q_stored[a.slot], 16)
                        sp.wait_ge(k_low_ready, a.index + 1)
                        for s in range(3):
                            sp.dma_start(kscr[a.slot, s], k_part[:, s]).then_inc(k_stored[a.slot], 16)
                    if d.valid():
                        sp.wait_ge(z_stored[d.slot], 16 * d.turn + 16)
                        rows = zscr[d.slot].rearrange("h q w -> (h q w)").rearrange("(r n) -> r n", n=D)
                        sp.dma_start(z_in[:, d.slot], rows).then_inc(z_loaded[d.slot], 16)
                    if a.valid():
                        sp.wait_ge(q_stored[a.slot], 48 * a.turn + 48)
                        for g, s in enumerate(QPART):
                            src = qscr[a.slot, s].rearrange("(h d) t k -> d t h k", d=DH)
                            dst = q_stack[16 * g:16 * g + 16, a.slot].rearrange("d (t h) k -> d t h k", t=2)
                            sp.dma_start(dst, src).then_inc(q_stacked[a.slot], 16)
                        sp.wait_ge(k_stored[a.slot], 48 * a.turn + 48)
                        for g, s in enumerate(PROD):
                            src = kscr[a.slot, s].rearrange("(h d) t k -> d t h k", d=DH)
                            dst = k_stack[16 * g:16 * g + 16, a.slot, :, 0:KEYS].rearrange("d (t h) k -> d t h k", t=2)
                            sp.dma_start(dst, src).then_inc(k_stacked[a.slot], 16)
                    if m.valid():
                        sp.wait_ge(m_step, M_STEPS * m.index + M_STEPS)
                        for s in range(3):
                            sp.dma_start(q_stack[ROWS + s:ROWS + s + 1, m.slot], m_part[:, s]).then_inc(m_stacked[m.slot], 16)

                sp.wait_ge(memsets, 5)
                pipeline(sp, iteration)
                for k in range(3):
                    sp.wait_ge(zf_stored[k], 16 * len(range(k, B, 3)))

            @blk.gpsimd
            def _(pool):
                for n, (dst, fill) in enumerate(((ct[:, :, :, KEYS:KPAD], 0.0), (k_stack[:, :, :, KEYS:KPAD], 0.0),
                                                 (k_stack[ROWS:128, :, :, 0:KEYS], 1.0), (v_aug[:, :, :, DH:32], 0.0),
                                                 (v_aug[:, :, :, DH:DH + 1], 1.0))):
                    nc.gpsimd.memset(dst, fill).then_inc(memsets, 1)
                    pool.wait_ge(memsets, n + 1)
                nc.gpsimd.memset(half[:], -0.5).then_inc(memsets, 1)
                pool.wait_ge(memsets, 6)
                for e in range(E):
                    pool.dma_start(w1_s[:, :, e, :], w1[e].rearrange("(c p) f -> p c f", p=128)).then_inc(w1_loaded, 16)
                g = nc.gpsimd

                def iteration(turn, i):
                    e = Batch(turn, i - 2)
                    if not e.valid():
                        return
                    n = POOL_STEPS * e.index
                    for k in range(3):
                        pool.wait_ge(norm_ready, 3 * e.index + k + 1)
                        g.tensor_tensor(rstd[:], var[:], half[:], ALU.pow).then_inc(rstd_ready, 1)
                        if k == 0:
                            pool.wait_ge(norm_ready_y, e.index + 1)
                            g.tensor_tensor(y[:], y[:], row_c[0][:], ALU.mult).then_inc(pool_step, 1)
                            pool.wait_ge(pool_step, n + 1)
                            g.tensor_tensor(y[:], y[:], row_c[1][:], ALU.add).then_inc(pool_step, 1)
                        elif k == 2:
                            pool.wait_ge(norm_ready_t, e.index + 1)
                            g.tensor_tensor(t1[:], t1[:], row_c[2][:], ALU.mult).then_inc(pool_step, 1)
                            pool.wait_ge(pool_step, n + 3)
                            after(pool, zft_done, e.index - 2)
                            after(pool, zf_stored[e.slot], 16 * e.turn)
                            g.tensor_tensor(zf_s[:, e.slot], t1[:], row_c[3][:], ALU.add).then_inc(zf_ready, 1)

                pipeline(pool, iteration, first=2)

            @blk.tensor
            def _(pe):
                def project(b, item):
                    if item == 0:
                        pe.wait_ge(d_ready, b.index + 1)
                        after(pe, v_biased, 2 * b.index - 1)
                        for c in range(2):
                            last = nc.tensor.transpose(pj[0][:, c * Q:c * Q + Q], drow[:, c * 128:c * 128 + 128], ident[0:Q, 0:Q])
                        last.then_inc(dt_done, 1)
                    elif item == 1:
                        pe.wait_ge(dt_copied, b.index + 1)
                        after(pe, v_biased, 2 * b.index)
                        for t in range(2):
                            for c in range(2):
                                last = nc.tensor.matmul(pj[1][:, t * Q:t * Q + Q], wq_s[:, c, t * 128:t * 128 + 128],
                                                        dt_s[:, c, :], start=(c == 0), stop=(c == 1))
                        last.then_inc(q_done, 1)
                    elif item < 4:
                        t = item - 2
                        if t == 0:
                            pe.wait_ge(ctx_loaded[b.slot], 16 * b.turn + 16)
                        else:
                            pe.wait_ge(q_rest_ready, 2 * b.index + 2)
                        for c in range(2):
                            last = nc.tensor.matmul(pj[t][:, 0:KEYS], wk_s[:, c, t * 128:t * 128 + 128],
                                                    ct[:, b.slot, c, 0:KEYS], start=(c == 0), stop=(c == 1))
                        last.then_inc(k_done, 1)
                    else:
                        n = item - 4
                        pe.wait_ge(k_rest_ready, 2 * b.index + 1 + n)
                        for kt in ((0, 1), (2,))[n]:
                            for c in range(2):
                                last = nc.tensor.matmul(pj[n][:, kt % 2 * D:kt % 2 * D + D], ct[:, b.slot, c, kt * 128:kt * 128 + 128],
                                                        wv_s[:, c, :], start=(c == 0), stop=(c == 1))
                        last.then_inc(v_done, 1)

                def score_rows(b, h):
                    if h == 0:
                        pe.wait_ge(q_stacked[b.slot], 96 * b.turn + 96)
                        pe.wait_ge(k_stacked[b.slot], 96 * b.turn + 96)
                    after(pe, max_done, H * b.index + h - 1)
                    nc.tensor.matmul(s_row[h % 2][0:Q, 0:KEYS], q_stack[0:ROWS, b.slot, h, :],
                                     k_stack[0:ROWS, b.slot, h, 0:KEYS], start=True, stop=True).then_inc(s_row_done, 1)

                def max_transposed(b):
                    pe.wait_ge(max_done, H * b.index + H)
                    after(pe, z_step, Z_STEPS * (b.index - 1))
                    after(pe, logits_ready, b.index - 3)
                    nc.tensor.transpose(tr[0:H, 0:Q], negmax[:], ident[0:Q, 0:Q]).then_inc(mt_done, 1)

                def scores(b, g):
                    if g == 0:
                        pe.wait_ge(m_stacked[b.slot], 48 * b.turn + 48)
                    after(pe, exp_done, NG * b.index + g - 1)
                    for j in range(4):
                        h, kt = 4 * (g // KT) + j, g % KT
                        last = nc.tensor.matmul(s_t[g % 2][:, j * Q:j * Q + Q], k_stack[0:MROWS, b.slot, h, kt * 128:kt * 128 + 128],
                                                q_stack[0:MROWS, b.slot, h, :], start=True, stop=True)
                    last.then_inc(s_t_done, 1)

                def values(b, g):
                    if g == 0:
                        pe.wait_ge(v_ready, b.index + 1)
                        after(pe, zt_copied, b.index)
                    pe.wait_ge(p_ready, NG * b.index + g + 1)
                    kt, grp = g % KT, g // KT
                    n = LAST if kt == KT - 1 else 128
                    for j in range(4):
                        last = nc.tensor.matmul(zt[32 * j:32 * j + 32, grp * Q:grp * Q + Q], v_aug[0:n, b.slot, kt * H + 4 * grp + j, :],
                                                p_t[0:n, g % 4, j * Q:j * Q + Q], start=(kt == 0), stop=(kt == KT - 1))
                    last.then_inc(pv_done, 1)

                def z_rows(b):
                    pe.wait_ge(zt_copied, b.index + 1)
                    if not (b.known and b.index == B - 1):
                        pe.wait_ge(m_step, M_STEPS * (b.index + 1) + M_STEPS)
                    after(pe, logits_ready, b.index - 2)
                    for grp in range(G):
                        last = nc.tensor.transpose(tr[0:Q, grp * 128:grp * 128 + 128], zt_s[:, grp * Q:grp * Q + Q], ident[:])
                    last.then_inc(zrow_done, 1)

                def zf_transposed(f, d):
                    pe.wait_ge(zf_ready, f.index + 1)
                    after(pe, z_step, Z_STEPS * (d.index + 1) if d.valid() else Z_STEPS * B)
                    after(pe, logits_ready, f.index)
                    for c in range(2):
                        last = nc.tensor.transpose(tr[:, c * Q:c * Q + Q], zf_s[:, f.slot, c * 128:c * 128 + 128], ident[0:Q, 0:Q])
                    last.then_inc(zft_done, 1)

                def router(f):
                    pe.wait_ge(zft_copied, f.index + 1)
                    for c in range(2):
                        last = nc.tensor.matmul(tr[0:Q, 256:256 + E], zft[:, c * Q:c * Q + Q], rw_s[:, c, :], start=(c == 0), stop=(c == 1))
                    last.then_inc(logits_done, 1)

                pe.wait_ge(const_loaded, 16 * N_CONST)
                pe.wait_ge(memsets, 5)

                def iteration(turn, i):
                    a, b, c, d, f = (Batch(turn, i + k) for k in (2, 1, 0, -1, -3))
                    for s in range(NG + 2):
                        if c.valid() and s < NG:
                            scores(c, s)
                        if c.valid() and s >= 2:
                            values(c, s - 2)
                        if b.valid() and s < 8:
                            score_rows(b, 2 * s)
                            score_rows(b, 2 * s + 1)
                        if a.valid() and s < 6:
                            project(a, s)
                        if d.valid() and s == 2:
                            z_rows(d)
                        if f.valid() and s == 5:
                            zf_transposed(f, d)
                        if f.valid() and s == 7:
                            router(f)
                        if b.valid() and s == 10:
                            max_transposed(b)

                pipeline(pe, iteration)

            @blk.scalar
            def _(act):
                def copy_parts(a, item):
                    if item == 0:
                        act.wait_ge(dt_done, a.index + 1)
                        after(act, q_done, a.index)
                        nc.scalar.activation(dt_s[:, :, :].rearrange("p c k -> p (c k)"), pj[0][:, 0:2 * Q], ACT.Copy).then_inc(dt_copied, 1)
                    elif item == 1:
                        act.wait_ge(q_done, a.index + 1)
                        before = Batch(a.turn if not a.known else 0, 0)
                        for t in range(2):
                            nc.scalar.activation(q_part[:, 0, t, :], pj[1][:, t * Q:t * Q + Q], ACT.Identity,
                                                 bias=bq_s[:, t:t + 1]).then_inc(qh_ready, 1)
                    elif item < 4:
                        t = item - 2
                        act.wait_ge(k_done, 2 * a.index + 1 + t)
                        nc.scalar.activation(k_part[:, 0, t, :], pj[t][:, 0:KEYS], ACT.Identity,
                                             bias=bk_s[:, t:t + 1]).then_inc(kh_ready, 1)
                    elif item == 4:
                        act.wait_ge(q_rest_ready, 2 * a.index + 2)
                        nc.scalar.activation(q_part[:, 1], q_rest[:], ACT.Copy).then_inc(qm_ready, 1)
                    elif item == 5:
                        act.wait_ge(k_rest_ready, 2 * a.index + 2)
                        nc.scalar.activation(k_part[:, 1], k_rest[:], ACT.Copy).then_inc(km_ready, 1)

                def exponentials(b, g):
                    act.wait_ge(s_t_done, NG * b.index + g + 1)
                    after(act, pv_done, NG * b.index + g - 3)
                    nc.scalar.activation(p_t[:, g % 4, :], s_t[g % 2][:, 0:4 * Q], ACT.Exp).then_inc(exp_done, 1)

                act.wait_ge(const_loaded, 16 * N_CONST)

                def iteration(turn, i):
                    a, p, c, d, f = (Batch(turn, i + k) for k in (2, 1, 0, -1, -3))
                    if d.valid():
                        act.wait_ge(pv_done, NG * d.index + NG)
                        after(act, zrow_done, d.index)
                        nc.scalar.activation(zt_s[:], zt[:, 0:G * Q], ACT.Copy).then_inc(zt_copied, 1)
                    for s in range(NG):
                        if c.valid():
                            exponentials(c, s)
                        if f.valid() and s == 5:
                            act.wait_ge(zft_done, f.index + 1)
                            nc.scalar.activation(zft[:], tr[:, 0:2 * Q], ACT.Copy).then_inc(zft_copied, 1)
                        if a.valid() and s < 6:
                            if s == 1 and p.valid():
                                act.wait_ge(q_stored[p.slot], 48 * p.turn + 48)
                                act.wait_ge(k_stored[p.slot], 48 * p.turn + 48)
                            copy_parts(a, s)

                pipeline(act, iteration)

            @blk.vector
            def _(dve):
                v = nc.vector
                dve.wait_ge(x_loaded[0], 16)
                dve.wait_ge(x_loaded[1], 16)
                dve.wait_ge(x_loaded[2], 16)
                dve.wait_ge(x_loaded[3], 16)
                dve.wait_ge(const_loaded, 16 * N_CONST)
                with dve.Fori(0, B) as b:
                    v.bn_stats(stats0[:, b, :], x_all[:, b, :]).then_inc(stats0_done, 1)
                dve.wait_ge(stats0_done, B)
                count = [0]

                def step0(ins):
                    count[0] += 1
                    ins.then_inc(ln0_step, 1)
                    dve.wait_ge(ln0_step, count[0])

                me, mo = stats0[:, :, 1], stats0[:, :, 4]
                step0(v.tensor_tensor(ln0[0][:], me, mo, ALU.add))
                step0(v.tensor_scalar(mean0[:], ln0[0][:], 0.5, None, ALU.mult))
                step0(v.tensor_tensor(ln0[0][:], me, mo, ALU.subtract))
                step0(v.tensor_tensor(ln0[1][:], ln0[0][:], ln0[0][:], ALU.mult))
                step0(v.tensor_tensor(ln0[2][:], stats0[:, :, 2], stats0[:, :, 5], ALU.add))
                step0(v.tensor_scalar(ln0[1][:], ln0[1][:], 0.25, EPS, ALU.mult, ALU.add))
                step0(v.tensor_scalar(ln0[2][:], ln0[2][:], 1.0 / D, None, ALU.mult))
                step0(v.tensor_tensor(ln0[0][:], ln0[2][:], ln0[1][:], ALU.add))

                def rsqrt(step, out_, var, a, b_):
                    step(v.tensor_scalar(a.bitcast(I32), var.bitcast(I32), 1, None, ALU.logical_shift_right))
                    step(v.tensor_scalar(out_.bitcast(I32), a.bitcast(I32), -1.0, float(MAGIC), ALU.mult, ALU.add))
                    for _ in range(3):
                        step(v.tensor_tensor(a, out_, out_, ALU.mult))
                        step(v.tensor_tensor(a, a, var, ALU.mult))
                        step(v.tensor_scalar(b_, a, -0.5, 1.5, ALU.mult, ALU.add))
                        step(v.tensor_tensor(out_, out_, b_, ALU.mult))

                rsqrt(step0, rstd0[:], ln0[0][:], ln0[1][:], ln0[2][:])

                def projections(a, item):
                    if item == 0:
                        after(dve, dt_done, a.index)
                        v.tensor_scalar(drow[:], x_all[:, a.index, :], mean0[:, bass.ds(a.index, 1)], rstd0[:, bass.ds(a.index, 1)],
                                        ALU.subtract, ALU.mult).then_inc(d_ready, 1)
                    elif item == 1:
                        for t in range(2):
                            dve.wait_ge(qh_ready, 2 * a.index + 2)
                            after(dve, q_low_ready, a.index)
                            v.scalar_tensor_tensor(q_rest[:, t], pj[1][:, t * Q:t * Q + Q], bq_s[:, t:t + 1], q_part[:, 0, t, :],
                                                   ALU.add, ALU.subtract).then_inc(q_rest_ready, 1)
                    elif item < 4:
                        t = item - 2
                        dve.wait_ge(kh_ready, 2 * a.index + 1 + t)
                        after(dve, k_low_ready, a.index)
                        v.scalar_tensor_tensor(k_rest[:, t], pj[t][:, 0:KEYS], bk_s[:, t:t + 1], k_part[:, 0, t, :],
                                               ALU.add, ALU.subtract).then_inc(k_rest_ready, 1)
                    elif item == 4:
                        dve.wait_ge(v_done, 2 * a.index + 1)
                        after(dve, v_ready, a.index)
                        bias2 = bv_s[:, :].unsqueeze(1).broadcast_to([128, 2, D])
                        v.tensor_tensor(v_raw[:, 0:2 * H, :].rearrange("p (t h) d -> p t (h d)", t=2), pj[0][:, :].rearrange("p (t n) -> p t n", t=2),
                                        bias2, ALU.add).then_inc(v_biased, 1)
                        dve.wait_ge(qm_ready, a.index + 1)
                        v.tensor_tensor(q_part[:, 2], q_rest[:], q_part[:, 1], ALU.subtract).then_inc(q_low_ready, 1)
                    elif item == 5:
                        dve.wait_ge(v_done, 2 * a.index + 2)
                        v.tensor_tensor(v_raw[:, 2 * H:3 * H, :].rearrange("p h d -> p (h d)"), pj[1][:, 0:D],
                                        bv_s[:, :], ALU.add).then_inc(v_biased, 1)
                        dve.wait_ge(km_ready, a.index + 1)
                        v.tensor_tensor(k_part[:, 2], k_rest[:], k_part[:, 1], ALU.subtract).then_inc(k_low_ready, 1)
                    elif item == 6:
                        dve.wait_ge(v_biased, 2 * a.index + 2)
                        v.tensor_scalar(v_neg[:], v_raw[:], 0.0, None, ALU.min).then_inc(v_neg_ready, 1)
                    elif item == 7:
                        dve.wait_ge(v_neg_ready, a.index + 1)
                        after(dve, pv_done, NG * (a.index - 2))
                        v.scalar_tensor_tensor(v_aug[:, a.slot, :, 0:DH], v_raw[:], 0.0, v_neg[:],
                                               ALU.max, ALU.add).then_inc(v_ready, 1)

                def row_max(b, h):
                    dve.wait_ge(s_row_done, H * b.index + h + 1)
                    if h == 0:
                        after(dve, mt_done, b.index)
                    v.tensor_reduce(negmax[:, h:h + 1], s_row[h % 2][0:Q, 0:KEYS], AXIS.X, ALU.max, negate=True).then_inc(max_done, 1)

                def max_parts(b):
                    n = M_STEPS * b.index
                    dve.wait_ge(mt_done, b.index + 1)
                    p = Batch(b.turn, b.slot - 1) if not b.known else Batch(0, b.index - 1)
                    if p.valid():
                        dve.wait_ge(m_stacked[p.slot], 48 * p.turn + 48)
                    v.tensor_copy(m_part[:, 0], tr[0:H, 0:Q]).then_inc(m_step, 1)
                    dve.wait_ge(m_step, n + 1)
                    v.tensor_tensor(m_rest[:], tr[0:H, 0:Q], m_part[:, 0], ALU.subtract).then_inc(m_step, 1)
                    dve.wait_ge(m_step, n + 2)
                    v.tensor_copy(m_part[:, 1], m_rest[:]).then_inc(m_step, 1)
                    dve.wait_ge(m_step, n + 3)
                    v.tensor_tensor(m_part[:, 2], m_rest[:], m_part[:, 1], ALU.subtract).then_inc(m_step, 1)

                def guard(b, g):
                    dve.wait_ge(exp_done, NG * b.index + g + 1)
                    v.tensor_scalar(p_t[:, g % 4, :], p_t[:, g % 4, :], 0.0, None, ALU.max).then_inc(p_ready, 1)

                def z_normalised(b):
                    heads = tr[0:Q, :].rearrange("q (h w) -> q h w", w=32)
                    n = Z_STEPS * b.index
                    dve.wait_ge(zrow_done, b.index + 1)
                    v.tensor_scalar(den[:], heads[:, :, DH], TINY, None, ALU.max).then_inc(z_step, 1)
                    dve.wait_ge(z_step, n + 1)
                    v.reciprocal(rden[:], den[:]).then_inc(z_step, 1)
                    dve.wait_ge(z_step, n + 2)
                    p = Batch(b.turn, b.slot - 1) if not b.known else Batch(0, b.index - 1)
                    if p.valid():
                        dve.wait_ge(z_stored[p.slot], 16 * p.turn + 16)
                    v.tensor_tensor(zn[:], heads[:, :, 0:DH], rden[:].unsqueeze(2).broadcast_to([Q, H, DH]),
                                    ALU.mult).then_inc(z_step, 1)

                def tail(b, part):
                    n = TAIL * b.index + TAIL_AT[part]
                    k = [n]

                    def step(ins):
                        k[0] += 1
                        ins.then_inc(tail_step, 1)
                        dve.wait_ge(tail_step, k[0])

                    def statistics(src):
                        step(v.bn_stats(st6[:], src))
                        v.tensor_copy(var[:], st6[:, 1:2])
                        step(v.bn_aggr(mv[:], st6[:]))
                        v.tensor_scalar(var[:], mv[:, 1:2], EPS, None, ALU.add).then_inc(norm_ready, 1)

                    xb = x_all[:, b.index, :]
                    if part == 0:
                        after(dve, zf_ready, b.index)
                        step(v.tensor_scalar(t1[:], xb, mean0[:, bass.ds(b.index, 1)], rstd0[:, bass.ds(b.index, 1)],
                                             ALU.subtract, ALU.mult))
                        dve.wait_ge(z_loaded[b.slot], 16 * b.turn + 16)
                        step(v.tensor_tensor(u[:], z_in[:, b.slot, :], t1[:], ALU.add))
                        statistics(u[:])
                    elif part == 1:
                        dve.wait_ge(rstd_ready, 3 * b.index + 1)
                        v.tensor_scalar(y[:], u[:], mv[:, 0:1], rstd[:], ALU.subtract, ALU.mult).then_inc(norm_ready_y, 1)
                    elif part == 2:
                        dve.wait_ge(pool_step, POOL_STEPS * b.index + 2)
                        step(v.tensor_tensor(y[:], y[:], xb, ALU.add))
                        statistics(y[:])
                    elif part == 3:
                        dve.wait_ge(rstd_ready, 3 * b.index + 2)
                        step(v.tensor_scalar(u[:], y[:], mv[:, 0:1], rstd[:], ALU.subtract, ALU.mult))
                        v.tensor_tensor(xb, y[:], u[:], ALU.add).then_inc(x2_step, 1)
                        statistics(u[:])
                    elif part == 4:
                        dve.wait_ge(rstd_ready, 3 * b.index + 3)
                        v.tensor_scalar(t1[:], u[:], mv[:, 0:1], rstd[:], ALU.subtract, ALU.mult).then_inc(norm_ready_t, 1)
                    assert part == 4 or k[0] == TAIL * b.index + TAIL_AT[part + 1] if b.known else True

                TAIL_AT = (0, 4, 4, 7, 10)
                TAIL = 10

                def add_logits(b):
                    dve.wait_ge(logits_done, b.index + 1)
                    v.tensor_tensor(logits[:, b.index, :], tr[0:Q, 256:256 + E], rb_s[:], ALU.add).then_inc(logits_ready, 1)

                def iteration(turn, i):
                    a, b, c, d, e, f = (Batch(turn, i + k) for k in (2, 1, 0, -1, -2, -3))
                    for s in range(NG):
                        if a.valid() and s == 0:
                            projections(a, 0)
                        if c.valid():
                            guard(c, s)
                        if b.valid() and s < 8:
                            row_max(b, 2 * s)
                            row_max(b, 2 * s + 1)
                        if a.valid() and 1 <= s < 8:
                            projections(a, s)
                        if b.valid() and s == 10:
                            max_parts(b)
                        if d.valid() and s == 3:
                            z_normalised(d)
                        if e.valid() and s in TAIL_SLOTS:
                            tail(e, TAIL_SLOTS.index(s))
                        if f.valid() and s == 8:
                            add_logits(f)

                pipeline(dve, iteration)

        ffn = ExitStack()
        with ffn:
            w2_s = sb(ffn, "w2_s", [128, 4, E, D])
            b1_s = sb(ffn, "b1_s", [128, E, HF])
            b2_s = sb(ffn, "b2_s", [128, E, D])
            cst = sb(ffn, "cst", [Q, E + B + 128 + B])
            sums = sb(ffn, "sums", [Q, 2 * Q])
            rev, steps, lanes, token = cst[:, 0:E], cst[:, E:E + B], cst[:, E + B:E + B + 128], cst[:, E + B + 128:]
            pr = sb(ffn, "pr", [Q, B, E])
            big = [sb(ffn, f"big{k}", [Q, B, E]) for k in range(2)]
            choice = sb(ffn, "choice", [Q, 2, B, E])
            cum = [sb(ffn, f"cum{k}", [Q, 16 + B, E]) for k in range(2)]
            col = [sb(ffn, f"col{k}", [Q, B]) for k in range(4)]
            wt = sb(ffn, "wt", [Q, 2, B])
            pos = sb(ffn, "pos", [Q, 2, B])
            pos_i = [sb(ffn, f"pos_i{k}", [Q, 2, B], I32) for k in range(3)]
            lane = sb(ffn, "lane", [Q, 2, B])
            tile_of = sb(ffn, "tile_of", [Q, 2, B])
            code = sb(ffn, "code", [Q, 2, B])
            over = sb(ffn, "over", [Q, E, B])
            ends = [sb(ffn, f"ends{k}", [Q, 4 + E]) for k in range(2)]
            first = sb(ffn, "first", [Q, E])
            past = sb(ffn, "past", [Q, NT, E])
            te = sb(ffn, "te", [Q, NT])
            te_i = sb(ffn, "te_i", [Q, NT], I32)
            lane_hot = sb(ffn, "lane_hot", [Q, 2, CH, 128])
            tile_hot = sb(ffn, "tile_hot", [Q, 2, CH, NT])
            picked = sb(ffn, "picked", [Q, 2, CH, 2, NT])
            slot_c = sb(ffn, "slot_c", [128, 2, NT])
            idx_t = [sb(ffn, f"idx_t{k}", [128, NT]) for k in range(2)]
            idx_g = sb(ffn, "idx_g", [128, 2], U32)
            idx_s = sb(ffn, "idx_s", [128, 2], U32)
            zg = sb(ffn, "zg", [128, 2, D])
            zgt = sb(ffn, "zgt", [128, 2, 2 * 128])
            hid = sb(ffn, "hid", [128, 2, HF])
            hidt = sb(ffn, "hidt", [128, 2, HF])
            yb = sb(ffn, "yb", [128, 2, D])
            ys = sb(ffn, "ys", [128, 2, D])

            p_zt = pb(ffn, "p_zt", [128, 512])
            p_h = [pb(ffn, f"p_h{k}", [128, 512]) for k in range(2)]
            p_ht = [pb(ffn, f"p_ht{k}", [128, 512]) for k in range(2)]
            p_y = [pb(ffn, f"p_y{k}", [128, 512]) for k in range(2)]
            p_r = pb(ffn, "p_r", [128, 512])

            w2_loaded, cst_loaded, x2_stored = sem("w2_loaded"), sem("cst_loaded"), sem("x2_stored")
            route_step, exp_ready, picks_ready, sums_done, picked_done = (sem(k) for k in ("route_step", "exp_ready", "picks_ready", "sums_done", "picked_done"))
            tiles_known = sem("tiles_known")
            idx_g_ready, idx_s_ready = sem("idx_g_ready"), sem("idx_s_ready")
            gathered = [sem(f"gathered{k}") for k in range(2)]
            scattered = [sem(f"scattered{k}") for k in range(2)]
            zgt_done, zgt_copied, up_done, biased, gelu_done = (sem(k) for k in ("zgt_done", "zgt_copied", "up_done", "biased", "gelu_done"))
            ht_done, ht_copied, down_done, yb_ready, y_ready = (sem(k) for k in ("ht_done", "ht_copied", "down_done", "yb_ready", "y_ready"))

            blk = ffn.enter_context(nc.Block())

            @blk.sync
            def _(sp):
                sp.dma_start(cst[:], route_c).then_inc(cst_loaded, 16)
                sp.dma_start(sums[:], sum_c).then_inc(cst_loaded, 16)
                for e in range(E):
                    sp.dma_start(w2_s[:, :, e, :], w2[e].rearrange("(c p) f -> p c f", p=128)).then_inc(w2_loaded, 16)
                sp.dma_start(b1_s[:], b1.unsqueeze(0).broadcast_to([128, E, HF])).then_inc(w2_loaded, 16)
                sp.dma_start(b2_s[:], b2.unsqueeze(0).broadcast_to([128, E, D])).then_inc(w2_loaded, 16)

            N_W2 = 16 * (E + 2)

            def tiles(eng, step):
                for k in range(2):
                    step(Tile(0, k))
                with eng.Fori(1, (NT - 3) // 2) as turn:
                    for r in range(2):
                        step(Tile(turn, r))
                for k in range(NT - 3, NT):
                    step(Tile(0, k))

            @blk.tensor
            def _(pe):
                pe.wait_ge(cst_loaded, 32)
                pe.wait_ge(picks_ready, 1)
                big0 = big[0][:].rearrange("q b e -> q (b e)")
                nc.tensor.matmul(p_r[0:Q, 0:B * E], sums[:, 0:Q], big0, start=True, stop=True)
                nc.tensor.matmul(p_r[0:Q, B * E:2 * B * E], sums[:, Q:2 * Q], big0, start=True, stop=True).then_inc(sums_done, 1)
                for n in range(2 * B):
                    if n % CH == 0:
                        pe.wait_ge(picks_ready, 2 + n // CH)
                    last = nc.tensor.matmul(p_y[0][:, 0:2 * NT], lane_hot[:, n // CH % 2, n % CH, :],
                                            picked[:, n // CH % 2, n % CH].rearrange("q a t -> q (a t)"),
                                            start=(n == 0), stop=(n == 2 * B - 1))
                    if n % CH == CH - 1:
                        last.then_inc(picked_done, 1)

                def up(k):
                    pe.wait_ge(gathered[k.slot], 16 * k.turn + 16)
                    after(pe, zgt_copied, k.index)
                    for c in range(2):
                        last = nc.tensor.transpose(p_zt[:, c * 128:c * 128 + 128], zg[:, k.slot, c * 128:c * 128 + 128], ident[:])
                    last.then_inc(zgt_done, 1)
                    e = pe.value_load(te_i[0:1, bass.ds(k.index, 1)], min_val=0, max_val=E - 1)
                    pe.wait_ge(zgt_copied, k.index + 1)
                    after(pe, biased, k.index - 1)
                    for c in range(2):
                        last = nc.tensor.matmul(p_h[k.slot][:], zgt[:, k.slot, c * 128:c * 128 + 128], w1_s[:, c, bass.ds(e, 1), :].rearrange("p e f -> p (e f)"),
                                                start=(c == 0), stop=(c == 1))
                    last.then_inc(up_done, 1)

                def step(k):
                    if not (k.known and k.index == NT - 1):
                        up(k.next())
                    pe.wait_ge(gelu_done, k.index + 1)
                    after(pe, ht_copied, k.index - 1)
                    for c in range(4):
                        last = nc.tensor.transpose(p_ht[k.slot][:, c * 128:c * 128 + 128], hid[:, k.slot, c * 128:c * 128 + 128], ident[:])
                    last.then_inc(ht_done, 1)
                    e = pe.value_load(te_i[0:1, bass.ds(k.index, 1)], min_val=0, max_val=E - 1)
                    pe.wait_ge(ht_copied, k.index + 1)
                    after(pe, yb_ready, k.index - 1)
                    for c in range(4):
                        last = nc.tensor.matmul(p_y[k.slot][:, 0:D], hidt[:, k.slot, c * 128:c * 128 + 128], w2_s[:, c, bass.ds(e, 1), :].rearrange("p e f -> p (e f)"),
                                                start=(c == 0), stop=(c == 3))
                    last.then_inc(down_done, 1)

                pe.wait_ge(tiles_known, 1)
                pe.wait_ge(w2_loaded, N_W2)
                pe.wait_ge(w1_loaded, 16 * E)
                up(Tile(0, 0))
                tiles(pe, step)

            @blk.scalar
            def _(act):
                act.wait_ge(route_step, 2)
                nc.scalar.activation(pr[:].rearrange("q b e -> q (b e)"), big[1][:].rearrange("q b e -> q (b e)"), ACT.Exp).then_inc(exp_ready, 1)

                def up(k):
                    act.wait_ge(zgt_done, k.index + 1)
                    after(act, up_done, k.index - 1)
                    nc.scalar.activation(zgt[:, k.slot], p_zt[:, 0:256], ACT.Copy).then_inc(zgt_copied, 1)

                def gelu(k):
                    act.wait_ge(biased, k.index + 1)
                    nc.scalar.activation(hid[:, k.slot], hid[:, k.slot], ACT.Gelu).then_inc(gelu_done, 1)

                def step(k):
                    more = not (k.known and k.index == NT - 1)
                    if more:
                        up(k.next())
                    act.wait_ge(ht_done, k.index + 1)
                    after(act, down_done, k.index - 1)
                    nc.scalar.activation(hidt[:, k.slot], p_ht[k.slot][:], ACT.Copy).then_inc(ht_copied, 1)
                    if more:
                        gelu(k.next())

                up(Tile(0, 0))
                gelu(Tile(0, 0))
                tiles(act, step)

            @blk.gpsimd
            def _(pool):
                gathers = [pool.alloc_register(f"gathers{k}") for k in range(2)]
                scatters = [pool.alloc_register(f"scatters{k}") for k in range(2)]
                pool.reg_mov(gathers[0], 1)
                pool.reg_mov(scatters[0], 1)
                zf_rows = zf_d.rearrange("b q d -> (b q) d")

                def gather(k):
                    pool.wait_ge(idx_g_ready, k.index + 1 if k.known else gathers[k.slot])
                    pool.reg_add(gathers[1 - k.slot], gathers[k.slot], 1)
                    pool.indirect_dma_start(zg[:, k.slot, :], None, zf_rows, bass.IndirectOffsetOnAxis(idx_g[:, k.slot:k.slot + 1], 0),
                                            bounds_check=B * Q - 1).then_inc(gathered[k.slot], 16)

                gather(Tile(0, 0))
                gather(Tile(0, 1))

                def step(k):
                    if not k.known or k.index + 2 < NT:
                        gather(k.next().next())
                    pool.wait_ge(y_ready, k.index + 1 if k.known else scatters[k.slot])
                    pool.reg_add(scatters[1 - k.slot], scatters[k.slot], 1)
                    pool.indirect_dma_start(y_d, bass.IndirectOffsetOnAxis(idx_s[:, k.slot:k.slot + 1], 0), ys[:, k.slot, :], None,
                                            bounds_check=2 * B * Q - 1, oob_is_err=False).then_inc(scattered[k.slot], 16)

                tiles(pool, step)
                for s in range(2):
                    pool.wait_ge(scattered[s], 16 * len(range(s, NT, 2)))

            @blk.vector
            def _(dve):
                v = nc.vector
                n = [0]

                def step(ins):
                    n[0] += 1
                    ins.then_inc(route_step, 1)
                    dve.wait_ge(route_step, n[0])

                def over_e(t):
                    return t.unsqueeze(2).broadcast_to([Q, B, E])

                revb = rev.unsqueeze(1).broadcast_to([Q, B, E])
                step(v.tensor_reduce(col[0][:], logits[:], AXIS.X, ALU.max))
                step(v.tensor_tensor(big[1][:], logits[:], over_e(col[0][:]), ALU.subtract))
                dve.wait_ge(exp_ready, 1)
                dve.wait_ge(cst_loaded, 32)
                step(v.tensor_reduce(col[0][:], pr[:], AXIS.X, ALU.add))
                step(v.reciprocal(col[1][:], col[0][:]))
                step(v.tensor_tensor(pr[:], pr[:], over_e(col[1][:]), ALU.mult))
                step(v.tensor_copy(big[0][:], pr[:]))
                for c in range(2):
                    step(v.tensor_reduce(wt[:, c], big[0][:], AXIS.X, ALU.max))
                    step(v.tensor_tensor(big[1][:], big[0][:], over_e(wt[:, c]), ALU.is_equal))
                    step(v.tensor_tensor(big[1][:], big[1][:], revb, ALU.mult))
                    step(v.tensor_reduce(col[c][:], big[1][:], AXIS.X, ALU.max))
                    step(v.tensor_tensor(choice[:, c], revb, over_e(col[c][:]), ALU.is_equal))
                    if c == 0:
                        step(v.scalar_tensor_tensor(big[0][:], choice[:, 0], -2.0, pr[:], ALU.mult, ALU.add))
                step(v.tensor_tensor(big[0][:], choice[:, 0], choice[:, 1], ALU.add))
                v.tensor_copy(col[3][:], wt[:, 0]).then_inc(picks_ready, 1)
                step(v.tensor_tensor(col[0][:], wt[:, 0], wt[:, 1], ALU.add))
                step(v.tensor_scalar(col[0][:], col[0][:], 1e-8, None, ALU.max))
                step(v.reciprocal(col[1][:], col[0][:]))
                for c in range(2):
                    step(v.tensor_tensor(wt[:, c], wt[:, c], col[1][:], ALU.mult))
                dve.wait_ge(sums_done, 1)
                for k in range(2):
                    step(v.memset(cum[k][:, 0:16, :], 0.0))
                    step(v.memset(ends[k][:, 0:4], 0.0))
                step(v.tensor_copy(cum[0][:, 16:, :].rearrange("q b e -> q (b e)"), p_r[0:Q, B * E:2 * B * E]))
                at = 0
                for k in (1, 2, 4, 8, 16):
                    step(v.tensor_tensor(cum[1 - at][:, 16:, :], cum[at][:, 16:, :], cum[at][:, 16 - k:16 + B - k, :], ALU.add))
                    at = 1 - at
                count = cum[at][:, 15 + B, :]
                step(v.tensor_tensor(over[:], count.unsqueeze(2).broadcast_to([Q, E, B]), steps.unsqueeze(1).broadcast_to([Q, E, B]), ALU.is_gt))
                step(v.tensor_reduce(ends[0][:, 4:], over[:], AXIS.X, ALU.add))
                en = 0
                for k in (1, 2, 4):
                    step(v.tensor_tensor(ends[1 - en][:, 4:], ends[en][:, 4:], ends[en][:, 4 - k:4 + E - k], ALU.add))
                    en = 1 - en
                step(v.tensor_scalar(first[:], ends[en][:, 3:3 + E], 128.0, None, ALU.mult))
                step(v.tensor_tensor(past[:], lanes[:, 0:NT].unsqueeze(2).broadcast_to([Q, NT, E]),
                                     ends[en][:, 4:].unsqueeze(1).broadcast_to([Q, NT, E]), ALU.is_ge))
                step(v.tensor_reduce(te[:], past[:], AXIS.X, ALU.add))
                step(v.tensor_scalar(te_i[:], te[:], float(E - 1), None, ALU.min))
                step(v.tensor_tensor(big[1][:], cum[at][:, 15:15 + B, :], first[:].unsqueeze(1).broadcast_to([Q, B, E]), ALU.add))
                step(v.tensor_tensor(big[1][:].rearrange("q b e -> q (b e)"), p_r[0:Q, 0:B * E], big[1][:].rearrange("q b e -> q (b e)"), ALU.add))
                for c in range(2):
                    step(v.tensor_tensor(pr[:], big[1][:], choice[:, c], ALU.mult))
                    step(v.tensor_reduce(pos[:, c], pr[:], AXIS.X, ALU.add))
                    step(v.tensor_scalar(code[:, c], token, float(c * B * Q), None, ALU.add))
                step(v.tensor_copy(pos_i[0][:], pos[:]))
                step(v.tensor_scalar(pos_i[1][:], pos_i[0][:], 7, None, ALU.logical_shift_right))
                step(v.tensor_scalar(pos_i[2][:], pos_i[0][:], 127, None, ALU.bitwise_and))
                step(v.tensor_copy(tile_of[:], pos_i[1][:]))
                step(v.tensor_copy(lane[:], pos_i[2][:]))
                for m in range(2 * B // CH):
                    c, b0, h = m * CH // B, m * CH % B, m % 2

                    def part(t, w):
                        return t[:, c, b0:b0 + CH].unsqueeze(2).broadcast_to([Q, CH, w])

                    if m >= 2:
                        dve.wait_ge(picked_done, m - 1)
                    step(v.tensor_tensor(tile_hot[:, h], lanes[:, 0:NT].unsqueeze(1).broadcast_to([Q, CH, NT]), part(tile_of, NT), ALU.is_equal))
                    step(v.tensor_tensor(picked[:, h, :, 0, :], tile_hot[:, h], part(code, NT), ALU.mult))
                    step(v.tensor_tensor(picked[:, h, :, 1, :], tile_hot[:, h], part(wt, NT), ALU.mult))
                    v.tensor_tensor(lane_hot[:, h], lanes.unsqueeze(1).broadcast_to([Q, CH, 128]), part(lane, 128), ALU.is_equal).then_inc(picks_ready, 1)
                dve.wait_ge(picked_done, 2 * B // CH)
                step(v.tensor_copy(slot_c[:].rearrange("p a t -> p (a t)"), p_y[0][:, 0:2 * NT]))
                cd = slot_c[:, 0]
                step(v.tensor_scalar(idx_t[0][:], cd, float(B * Q), -float(B * Q), ALU.is_gt, ALU.mult))
                step(v.tensor_tensor(idx_t[0][:], idx_t[0][:], cd, ALU.add))
                step(v.tensor_scalar(idx_t[0][:], idx_t[0][:], -1.0, 0.0, ALU.add, ALU.max))
                step(v.tensor_scalar(idx_t[1][:], cd, 0.0, float(4 * B * Q), ALU.is_equal, ALU.mult))
                step(v.tensor_tensor(idx_t[1][:], idx_t[1][:], cd, ALU.add))
                step(v.tensor_scalar(idx_t[1][:], idx_t[1][:], -1.0, None, ALU.add))
                v.tensor_copy(past[:, 0, :], past[:, 1, :]).then_inc(tiles_known, 1)

                def to_gather(k):
                    v.tensor_scalar(idx_g[:, k.slot:k.slot + 1], idx_t[0][:, bass.ds(k.index, 1)], 0.0, None, ALU.add).then_inc(idx_g_ready, 1)

                def bias(k):
                    e = dve.value_load(te_i[0:1, bass.ds(k.index, 1)], min_val=0, max_val=E - 1)
                    dve.wait_ge(up_done, k.index + 1)
                    after(dve, ht_done, k.index - 1)
                    v.tensor_tensor(hid[:, k.slot], p_h[k.slot][:], b1_s[:, bass.ds(e, 1), :].rearrange("p e f -> p (e f)"), ALU.add).then_inc(biased, 1)

                def tile_step(k):
                    if not k.known or k.index + 2 < NT:
                        dve.wait_ge(zgt_done, k.index + 1)
                        to_gather(k.next().next())
                    if not (k.known and k.index == NT - 1):
                        bias(k.next())
                    e = dve.value_load(te_i[0:1, bass.ds(k.index, 1)], min_val=0, max_val=E - 1)
                    after(dve, scattered[k.slot], 16 * k.turn)
                    v.tensor_scalar(idx_s[:, k.slot:k.slot + 1], idx_t[1][:, bass.ds(k.index, 1)], 0.0, None, ALU.add).then_inc(idx_s_ready, 1)
                    dve.wait_ge(down_done, k.index + 1)
                    v.tensor_tensor(yb[:, k.slot], p_y[k.slot][:, 0:D], b2_s[:, bass.ds(e, 1), :].rearrange("p e f -> p (e f)"), ALU.add).then_inc(yb_ready, 1)
                    dve.wait_ge(yb_ready, k.index + 1)
                    dve.wait_ge(idx_s_ready, k.index + 1)
                    v.tensor_scalar(ys[:, k.slot], yb[:, k.slot], slot_c[:, 1, bass.ds(k.index, 1)], None, ALU.mult).then_inc(y_ready, 1)

                dve.wait_ge(w2_loaded, N_W2)
                to_gather(Tile(0, 0))
                to_gather(Tile(0, 1))
                bias(Tile(0, 0))
                tiles(dve, tile_step)

        end = ExitStack()
        with end:
            PARTS = 4
            W = B // PARTS
            y1 = [[sb(end, f"y{c}_{k}", [Q, W, D]) for k in range(2)] for c in range(2)]
            y_loaded = [sem(f"y_loaded{k}") for k in range(PARTS)]
            sum_step = sem("sum_step")
            blk = end.enter_context(nc.Block())
            yv = y_d.rearrange("(c b q) d -> c q b d", c=2, q=Q)
            ov = out.rearrange("b q d -> q b d")

            @blk.sync
            def _(sp):
                for m in range(PARTS):
                    if m >= 2:
                        sp.wait_ge(sum_step, 2 * m - 2)
                    for c in range(2):
                        sp.dma_start(y1[c][m % 2][:], yv[c, :, m * W:m * W + W]).then_inc(y_loaded[m], 16)

            @blk.scalar
            def _(act):
                for m in range(PARTS):
                    act.wait_ge(sum_step, 2 * m + 2)
                    act.dma_start(ov[:, m * W:m * W + W], x_all[:, m * W:m * W + W]).then_inc(out_stored, 16)
                act.wait_ge(out_stored, 16 * PARTS)

            @blk.vector
            def _(dve):
                for m in range(PARTS):
                    dve.wait_ge(y_loaded[m], 32)
                    nc.vector.tensor_tensor(y1[0][m % 2][:], y1[0][m % 2][:], y1[1][m % 2][:], ALU.add).then_inc(sum_step, 1)
                    dve.wait_ge(sum_step, 2 * m + 1)
                    xm = x_all[:, m * W:m * W + W]
                    nc.vector.tensor_tensor(xm, xm, y1[0][m % 2][:], ALU.add).then_inc(sum_step, 1)


TAIL_SLOTS = (0, 2, 5, 7, 9)


def kernel(**inputs):
    import numpy as np
    import concourse.bacc as bacc
    from concourse.bass_utils import run_bass_kernel_spmd

    def lay(w):
        return np.ascontiguousarray(np.asarray(w).T.reshape(2, 128, D).transpose(1, 0, 2))

    p = {k.replace("L0_", ""): np.asarray(v) for k, v in inputs.items()}
    ctx = p["ctx_1024"]
    arrays = {
        "x": p["x"],
        "ctx_t": np.ascontiguousarray(ctx.transpose(0, 2, 1).reshape(B, 2, 128, KEYS).transpose(0, 2, 1, 3)),
        "wq_t": lay(p["xattn_Wq"]), "bq": p["xattn_bq"].reshape(2, 128).T,
        "wk_t": lay(p["xattn_Wk"]), "bk": p["xattn_bk"].reshape(2, 128).T,
        "wv_t": lay(p["xattn_Wv"]), "bv": p["xattn_bv"],
        "gamma": p["xattn_gamma"], "beta": p["xattn_beta"],
        "ln_g": p["ffn_ln_g"], "ln_b": p["ffn_ln_b"], "rw": p["ffn_rW"], "rb": p["ffn_rb"],
        "w1": p["ffn_W1"], "b1": p["ffn_b1"], "w2": p["ffn_W2"], "b2": p["ffn_b2"],
        "ident_d": np.eye(128, dtype=np.float32),
        "route_c": np.concatenate([np.tile(np.concatenate([np.arange(E, 0, -1), 128 * np.arange(B), np.arange(128)]), (Q, 1)),
                                   1 + np.arange(B) * Q + np.arange(Q)[:, None]], 1).astype(np.float32),
        "sum_c": np.concatenate([np.triu(np.ones((Q, Q)), 1), np.ones((Q, Q))], 1).astype(np.float32),
    }
    nc = bacc.Bacc("TRN2", target_bir_lowering=False, num_devices=1)
    args = {k: nc.dram_tensor("in_" + k, a.shape, mybir.dt.from_np(a.dtype), kind="ExternalInput").ap() for k, a in arrays.items()}
    args["kscr"] = nc.dram_tensor("kscr", [3, 3, 128, 2, KEYS], BF16, kind="Internal").ap()
    args["qscr"] = nc.dram_tensor("qscr", [3, 3, 128, 2, Q], BF16, kind="Internal").ap()
    args["zscr"] = nc.dram_tensor("zscr", [3, H, Q, DH], FP32, kind="Internal").ap()
    args["zf_d"] = nc.dram_tensor("zf_d", [B, Q, D], FP32, kind="Internal").ap()
    args["y_d"] = nc.dram_tensor("y_d", [2 * B * Q, D], FP32, kind="Internal").ap()
    args["out"] = nc.dram_tensor("out_x", [B, Q, D], FP32, kind="ExternalOutput").ap()
    build(nc, **args)
    r = run_bass_kernel_spmd(nc, [{"in_" + k: np.ascontiguousarray(a) for k, a in arrays.items()}], core_ids=[0])
    return r.results[0]["out_x"]
```

```python
import concourse.bass as bass
from concourse import mybir
from contextlib import ExitStack

FP32 = mybir.dt.float32
BF16 = mybir.dt.bfloat16
I32 = mybir.dt.int32
U32 = mybir.dt.uint32
ALU = mybir.AluOpType
ACT = mybir.ActivationFunctionType
AXIS = mybir.AxisListType

B, Q, D = 32, 100, 256
KEYS = 361
H, DH = 16, 16
E, HF = 8, 512
EPS = 1e-5
KT = 3
KPAD = KT * 128
LAST = KEYS - 2 * 128
PROD = [0, 0, 0, 1, 1, 2]
QPART = [0, 1, 2, 0, 1, 0]
ROWS = 16 * len(PROD)
MROWS = ROWS + 3
G = 4
NG = G * KT
TINY = 1e-30
SCORES_LAG, GUARD_LAG, VALUES_LAG = 4, 5, 7
NT = (2 * B * Q + E * 127) // 128
CH = 16


class Batch:

    def __init__(self, turn, c):
        self.index = turn * 3 + c if c or isinstance(turn, int) else turn * 3
        self.slot = c % 3
        self.turn = turn + c // 3 if c // 3 else turn
        self.known = isinstance(turn, int)

    def valid(self):
        return not self.known or 0 <= self.index < B


class Tile:

    def __init__(self, turn, c):
        self.known = isinstance(turn, int)
        self.base, self.c = turn, c
        self.index = turn * 2 + c if c or self.known else turn * 2
        self.slot = c % 2
        self.turn = turn + c // 2 if c // 2 else turn

    def later(self, n):
        return Tile(self.base, self.c + n)


def after(eng, sem, value):
    if isinstance(value, int) and value <= 0:
        return
    eng.wait_ge(sem, value)


def lagging(turn, i, s, lag):
    return Batch(turn, i + (s - lag) // NG), (s - lag) % NG


def pipeline(eng, iteration, first=1, last=10):
    for i in range(-2, 3 * first):
        iteration(0, i)
    with eng.Fori(first, last) as turn:
        for r in range(3):
            iteration(turn, r)
    for i in range(3 * last, 35):
        iteration(0, i)


def build(nc, x, ctx_t, wq_t, bq, wk_t, bk, wv_t, bv, gamma, beta, ln_g, ln_b, rw, rb, w1, b1, w2, b2,
          ident_d, route_c, sum_c, kscr, qscr, zscr, zf_d, y_d, out):
    es = ExitStack()
    with es:
        def sem(name):
            return es.enter_context(nc.semaphore(name))

        def sb(stack, name, shape, dt=FP32):
            return stack.enter_context(nc.sbuf_tensor(name, shape, dt))

        def pb(stack, name, shape, dt=FP32):
            return stack.enter_context(nc.psum_tensor(name, shape, dt))

        x_all = sb(es, "x_all", [Q, B, D])
        logits = sb(es, "logits", [Q, B, E])
        rw_s = sb(es, "rw_s", [128, 2, E])
        rb_s = sb(es, "rb_s", [Q, E])
        w1_s = sb(es, "w1_s", [128, 2, E, HF])
        ident = sb(es, "ident", [128, 128])
        mean0 = sb(es, "mean0", [Q, B])
        rstd0 = sb(es, "rstd0", [Q, B])

        x_loaded = [sem(f"x_loaded{k}") for k in range(4)]
        const_loaded = sem("const_loaded")
        N_CONST = 14
        w1_loaded = sem("w1_loaded")
        x2_step = sem("x2_step")
        memsets, pad_written, ones_written = sem("memsets"), sem("pad_written"), sem("ones_written")
        ln0_step = sem("ln0_step")
        stats0_done = sem("stats0_done")
        out_stored = sem("out_stored")

        wt = sb(es, "wt", [Q, 2, B])

        att = ExitStack()
        with att:
            stats0 = sb(att, "stats0", [Q, B, 6])
            ln0 = [sb(att, f"ln0_{k}", [Q, B]) for k in range(4)]
            ct = sb(att, "ct", [128, 3, 2, KPAD])
            wq_s = sb(att, "wq_s", [128, 2, D])
            wk_s = sb(att, "wk_s", [128, 2, D])
            wv_s = sb(att, "wv_s", [128, 2, D])
            bq_s = sb(att, "bq_s", [128, 2])
            bk_s = sb(att, "bk_s", [128, 2])
            bv_s = sb(att, "bv_s", [128, D])
            row_c = [sb(att, f"row_c{k}", [Q, D]) for k in range(4)]
            drow = sb(att, "drow", [Q, D])
            dt_s = sb(att, "dt_s", [128, 2, Q])
            q_part = sb(att, "q_part", [128, 2, 3, Q], BF16)
            q_rest = sb(att, "q_rest", [128, 2, Q])
            k_part = sb(att, "k_part", [128, 2, 3, KEYS], BF16)
            ones_row = sb(att, "ones_row", [MROWS - ROWS, KEYS], BF16)
            k_rest = sb(att, "k_rest", [128, 2, KEYS])
            k_stack = sb(att, "k_stack", [128, 3, H, KEYS], BF16)
            q_stack = sb(att, "q_stack", [128, 3, H, Q], BF16)
            v_raw = sb(att, "v_raw", [128, KT * H, DH])
            v_neg = sb(att, "v_neg", [128, KT * H, DH])
            v_aug = sb(att, "v_aug", [128, 3, KT * H, 32])
            negmax = sb(att, "negmax", [Q, H])
            m_part = sb(att, "m_part", [H, 3, Q], BF16)
            m_rest = sb(att, "m_rest", [H, Q])
            p_t = sb(att, "p_t", [128, 4, 4 * Q])
            zt_s = sb(att, "zt_s", [128, G * Q])
            den = sb(att, "den", [Q, H])
            rden = sb(att, "rden", [Q, H])
            zn = sb(att, "zn", [Q, H, DH])
            z_in = sb(att, "z_in", [Q, 3, D])
            u = sb(att, "u", [Q, D])
            y = sb(att, "y", [Q, D])
            t1 = sb(att, "t1", [Q, D])
            nmean = sb(att, "nmean", [Q, 1])
            nb = sb(att, "nb", [Q, 1])
            nb0 = sb(att, "nb0", [Q, B])
            td = sb(att, "td", [Q, D])
            xbeta = sb(att, "xbeta", [Q, D])
            v_pos = sb(att, "v_pos", [128, KT * H, DH])
            st6 = sb(att, "st6", [Q, 6])
            mv = sb(att, "mv", [Q, 2])
            var = sb(att, "var", [Q, 1])
            rstd = sb(att, "rstd", [Q, 1])
            half = sb(att, "half", [Q, 1])
            zf_s = sb(att, "zf_s", [Q, 3, D])
            zft = sb(att, "zft", [128, 2 * Q])

            s_row = [pb(att, f"s_row{k}", [128, 512]) for k in range(2)]
            s_t = [pb(att, f"s_t{k}", [128, 512]) for k in range(2)]
            pj = [pb(att, f"pj{k}", [128, 512]) for k in range(2)]
            zt = pb(att, "zt", [128, 512])
            tr = pb(att, "tr", [128, 512])

            ctx_loaded = [sem(f"ctx_loaded{k}") for k in range(3)]
            k_stored = [sem(f"k_stored{k}") for k in range(3)]
            q_stored = [sem(f"q_stored{k}") for k in range(3)]
            k_stacked = [sem(f"k_stacked{k}") for k in range(3)]
            q_stacked = [sem(f"q_stacked{k}") for k in range(3)]
            z_stored = [sem(f"z_stored{k}") for k in range(3)]
            z_loaded = [sem(f"z_loaded{k}") for k in range(3)]
            m_stacked = [sem(f"m_stacked{k}") for k in range(3)]
            d_ready, dt_done, dt_copied = sem("d_ready"), sem("dt_done"), sem("dt_copied")
            q_done, k_done, v_done = sem("q_done"), sem("k_done"), sem("v_done")
            qh_ready, qm_ready, kh_ready, km_ready = sem("qh_ready"), sem("qm_ready"), sem("kh_ready"), sem("km_ready")
            q_rest_ready, q_low_ready = sem("q_rest_ready"), sem("q_low_ready")
            k_rest_ready, k_low_ready = sem("k_rest_ready"), sem("k_low_ready")
            v_biased, v_neg_ready, v_ready = sem("v_biased"), sem("v_neg_ready"), sem("v_ready")
            s_row_done, max_done = sem("s_row_done"), sem("max_done")
            mt_done, m_step = sem("mt_done"), sem("m_step")
            s_t_done, exp_done, p_ready, pv_done = sem("s_t_done"), sem("exp_done"), sem("p_ready"), sem("pv_done")
            zt_copied, zrow_done, z_step, tail_step = sem("zt_copied"), sem("zrow_done"), sem("z_step"), sem("tail_step")
            zf_stored = [sem(f"zf_stored{k}") for k in range(3)]
            norm_ready, rstd_ready, pool_step, zf_ready = sem("norm_ready"), sem("rstd_ready"), sem("pool_step"), sem("zf_ready")
            norm_ready_y, u_normalised, norm_ready_t = sem("norm_ready_y"), sem("u_normalised"), sem("norm_ready_t")
            POOL_STEPS = 3
            u_ready, nb_ready = sem("u_ready"), sem("nb_ready")
            rstd0_ready, nb0_ready, td_ready, xbeta_ready = sem("rstd0_ready"), sem("nb0_ready"), sem("td_ready"), sem("xbeta_ready")
            zft_done, zft_copied, logits_done, logits_ready = sem("zft_done"), sem("zft_copied"), sem("logits_done"), sem("logits_ready")
            M_STEPS = 2
            m_high_ready, m_mid_ready = sem("m_high_ready"), sem("m_mid_ready")
            ROW_SLOTS, h = [], 0
            for n in ROW_COUNTS:
                ROW_SLOTS.append(tuple(range(h, h + n)))
                h += n
            
            Q_LOADS, K_LOADS = 16 * 3, 16 * len(PROD)
            Z_STEPS = 3

            blk = att.enter_context(nc.Block())

            @blk.sync
            def _(sp):
                xv = x.rearrange("b q d -> q b d")

                def load_x(k):
                    sp.dma_start(x_all[:, 8 * k:8 * k + 8, :], xv[:, 8 * k:8 * k + 8, :]).then_inc(x_loaded[k], 16)

                load_x(0)
                sp.dma_start(wk_s[:], wk_t).then_inc(const_loaded, 16)
                sp.wait_ge(pad_written, 1)
                sp.dma_start(ct[:, 0, :, 0:KEYS], ctx_t[0]).then_inc(ctx_loaded[0], 16)
                sp.dma_start(ident[:], ident_d).then_inc(const_loaded, 16)
                sp.dma_start(wq_s[:], wq_t).then_inc(const_loaded, 16)
                sp.dma_start(wv_s[:], wv_t).then_inc(const_loaded, 16)
                sp.dma_start(bq_s[:], bq).then_inc(const_loaded, 16)
                sp.dma_start(bk_s[:], bk).then_inc(const_loaded, 16)
                sp.dma_start(bv_s[:], bv.unsqueeze(0).broadcast_to([128, D])).then_inc(const_loaded, 16)
                for dst, src in zip(row_c, (gamma, beta, ln_g, ln_b)):
                    sp.dma_start(dst[:], src.unsqueeze(0).broadcast_to([Q, D])).then_inc(const_loaded, 16)
                sp.dma_start(rw_s[:], rw.rearrange("(c p) e -> p c e", p=128)).then_inc(const_loaded, 16)
                sp.dma_start(rb_s[:], rb.unsqueeze(0).broadcast_to([Q, E])).then_inc(const_loaded, 16)
                sp.wait_ge(ones_written, 1)
                sp.dma_start(k_stack[ROWS:MROWS].rearrange("r s h k -> r (s h) k"),
                             ones_row[:].unsqueeze(1).broadcast_to([MROWS - ROWS, 3 * H, KEYS])).then_inc(const_loaded, 16)
                for k in range(1, 4):
                    load_x(k)

                def iteration(turn, i):
                    n, a, m, d, f = (Batch(turn, i + k) for k in (3, 2, 1, -1, -3))
                    if f.valid():
                        sp.wait_ge(zf_ready, f.index + 1)
                        sp.dma_start(zf_d[f.index], zf_s[:, f.slot]).then_inc(zf_stored[f.slot], 16)
                    if n.valid():
                        after(sp, v_done, 2 * (n.index - 2))
                        sp.dma_start(ct[:, n.slot, :, 0:KEYS], ctx_t[n.index]).then_inc(ctx_loaded[n.slot], 16)
                    if a.valid():
                        sp.wait_ge(k_low_ready, a.index + 1)
                        sp.dma_start(kscr[a.slot].rearrange("t s r h k -> (r h) t s k"), k_part[:]).then_inc(k_stored[a.slot], 16)
                        sp.wait_ge(q_low_ready, a.index + 1)
                        sp.dma_start(qscr[a.slot].rearrange("t s r h k -> (r h) t s k"), q_part[:]).then_inc(q_stored[a.slot], 16)
                        after(sp, s_t_done, NG * (a.index - 2))
                        sp.wait_ge(k_stored[a.slot], 16 * a.turn + 16)
                        for g, s in enumerate(PROD):
                            dst = k_stack[16 * g:16 * g + 16, a.slot].rearrange("r (t h) k -> r t (h k)", t=2)
                            sp.dma_start(dst, kscr[a.slot, :, s].rearrange("t r h k -> r t (h k)")).then_inc(k_stacked[a.slot], 16)
                        sp.wait_ge(q_stored[a.slot], 16 * a.turn + 16)
                        row = 0
                        for n in (3, 2, 1):
                            dst = q_stack[16 * row:16 * (row + n), a.slot].rearrange("r (t h) k -> r t (h k)", t=2)
                            sp.dma_start(dst, qscr[a.slot, :, 0:n].rearrange("t s r h k -> (s r) t (h k)")).then_inc(q_stacked[a.slot], 16)
                            row += n
                    if d.valid():
                        sp.wait_ge(z_step, Z_STEPS * d.index + Z_STEPS)
                        sp.dma_start(zscr[d.slot].rearrange("h q w -> q h w"), zn[:]).then_inc(z_stored[d.slot], 16)
                    if m.valid():
                        sp.wait_ge(m_step, M_STEPS * m.index + M_STEPS)
                        for s in range(3):
                            sp.dma_start(q_stack[ROWS + s:ROWS + s + 1, m.slot], m_part[:, s]).then_inc(m_stacked[m.slot], 16)
                    if d.valid():
                        sp.wait_ge(z_stored[d.slot], 16 * d.turn + 16)
                        rows = zscr[d.slot].rearrange("h q w -> (h q w)").rearrange("(r n) -> r n", n=D)
                        sp.dma_start(z_in[:, d.slot], rows).then_inc(z_loaded[d.slot], 16)
                    if d.known and i >= 35 - E:
                        e = i - (35 - E)
                        sp.dma_start(w1_s[:, :, e, :], w1[e].rearrange("(c p) f -> p c f", p=128)).then_inc(w1_loaded, 16)

                pipeline(sp, iteration, last=9)
                for k in range(3):
                    sp.wait_ge(zf_stored[k], 16 * len(range(k, B, 3)))

            @blk.gpsimd
            def _(pool):
                for n, (dst, fill) in enumerate(((half[:], -0.5), (v_aug[:, :, :, DH:32], 0.0), (v_aug[:, :, :, DH:DH + 1], 1.0))):
                    nc.gpsimd.memset(dst, fill).then_inc(memsets, 1)
                    pool.wait_ge(memsets, n + 1)
                g = nc.gpsimd

                def inverse_deviation_x(k):
                    pool.wait_ge(ln0_step, 8 * (k + 1))
                    part = slice(8 * k, 8 * k + 8)
                    g.tensor_tensor(rstd0[:, part], ln0[0][:, part], half[:].broadcast_to([Q, 8]), ALU.pow).then_inc(rstd0_ready, 1)

                inverse_deviation_x(0)
                for k in range(4):
                    pool.wait_ge(x_loaded[k], 16)
                pool.wait_ge(const_loaded, 16 * N_CONST)

                def iteration(turn, i):
                    a, e = Batch(turn, i + 2), Batch(turn, i - 2)

                    def inverse_deviation(k):
                        pool.wait_ge(norm_ready, 6 * e.index + 2 * k + 2)
                        g.tensor_tensor(rstd[:], var[:], half[:], ALU.pow).then_inc(rstd_ready, 1)
                        pool.wait_ge(rstd_ready, 3 * e.index + k + 1)
                        g.tensor_tensor(nb[:], nmean[:], rstd[:], ALU.mult).then_inc(nb_ready, 1)

                    if e.valid():
                        pool.wait_ge(td_ready, e.index + 1)
                        pool.wait_ge(z_loaded[e.slot], 16 * e.turn + 16)
                        g.tensor_tensor(u[:], z_in[:, e.slot, :], td[:], ALU.add).then_inc(u_ready, 1)
                    if a.valid():
                        pool.wait_ge(km_ready, a.index + 1)
                        g.tensor_tensor(k_part[:, :, 2], k_rest[:], k_part[:, :, 1], ALU.subtract).then_inc(k_low_ready, 1)
                    if e.valid():
                        inverse_deviation(0)
                        g.tensor_tensor(xbeta[:], x_all[:, e.index, :], row_c[1][:], ALU.add).then_inc(xbeta_ready, 1)
                    if e.valid():
                        pool.wait_ge(norm_ready_y, e.index + 1)
                        g.tensor_tensor(y[:], y[:], row_c[0][:], ALU.mult).then_inc(pool_step, 1)
                        pool.wait_ge(xbeta_ready, e.index + 1)
                        pool.wait_ge(pool_step, POOL_STEPS * e.index + 1)
                        g.tensor_tensor(y[:], y[:], xbeta[:], ALU.add).then_inc(pool_step, 1)
                    if a.valid():
                        pool.wait_ge(qm_ready, a.index + 1)
                        g.tensor_tensor(q_part[:, :, 2], q_rest[:], q_part[:, :, 1], ALU.subtract).then_inc(q_low_ready, 1)
                    if e.valid():
                        inverse_deviation(1)
                    if e.valid():
                        inverse_deviation(2)
                        g.tensor_tensor(x_all[:, e.index, :], y[:], u[:], ALU.add).then_inc(x2_step, 1)
                        pool.wait_ge(norm_ready_t, e.index + 1)
                        g.tensor_tensor(t1[:], t1[:], row_c[2][:], ALU.mult).then_inc(pool_step, 1)
                        pool.wait_ge(pool_step, POOL_STEPS * e.index + 3)
                        after(pool, zft_done, e.index - 2)
                        after(pool, zf_stored[e.slot], 16 * e.turn)
                        g.tensor_tensor(zf_s[:, e.slot], t1[:], row_c[3][:], ALU.add).then_inc(zf_ready, 1)
                    if a.valid():
                        after(pool, pv_done, NG * (a.index - 2))
                        pool.wait_ge(v_neg_ready, 2 * a.index + 2)
                        g.tensor_tensor(v_aug[:, a.slot, :, 0:DH], v_pos[:], v_neg[:], ALU.add).then_inc(v_ready, 1)
                    for k in X_ROUNDS.get(i, ()) if a.known else ():
                        inverse_deviation_x(k)

                pipeline(pool, iteration, first=2)

            @blk.tensor
            def _(pe):
                def project(b, item):
                    if item < 4:
                        t, c = item // 2, item % 2
                        if item == 0:
                            pe.wait_ge(ctx_loaded[b.slot], 16 * b.turn + 16)
                            after(pe, v_biased, 2 * b.index)
                        last = nc.tensor.matmul(pj[t][:, 0:KEYS], wk_s[:, c, t * 128:t * 128 + 128],
                                                ct[:, b.slot, c, 0:KEYS], start=(c == 0), stop=(c == 1))
                        if c == 1:
                            last.then_inc(k_done, 1)
                    elif item == 4:
                        pe.wait_ge(d_ready, b.index + 1)
                        pe.wait_ge(k_rest_ready, 2 * b.index + 1)
                        for c in range(2):
                            last = nc.tensor.transpose(pj[0][:, c * Q:c * Q + Q], drow[:, c * 128:c * 128 + 128], ident[0:Q, 0:Q])
                        last.then_inc(dt_done, 1)
                    elif item < 7:
                        t = item - 5
                        if t == 0:
                            pe.wait_ge(dt_copied, b.index + 1)
                        for c in range(2):
                            last = nc.tensor.matmul(pj[0][:, t * Q:t * Q + Q], wq_s[:, c, t * 128:t * 128 + 128],
                                                    dt_s[:, c, :], start=(c == 0), stop=(c == 1))
                        if t == 1:
                            last.then_inc(q_done, 1)
                    else:
                        kt = item - 7
                        if kt == 0:
                            pe.wait_ge(k_rest_ready, 2 * b.index + 2)
                        elif kt == 2:
                            pe.wait_ge(q_rest_ready, 2 * b.index + 2)
                        bank = pj[1 - kt // 2]
                        for c in range(2):
                            last = nc.tensor.matmul(bank[:, kt % 2 * D:kt % 2 * D + D], ct[:, b.slot, c, kt * 128:kt * 128 + 128],
                                                    wv_s[:, c, :], start=(c == 0), stop=(c == 1))
                        if kt > 0:
                            last.then_inc(v_done, 1)

                def score_rows(b, h):
                    if h == 0:
                        pe.wait_ge(q_stacked[b.slot], Q_LOADS * b.turn + Q_LOADS)
                        pe.wait_ge(k_stacked[b.slot], K_LOADS * b.turn + K_LOADS)
                    after(pe, max_done, H * b.index + h - 1)
                    nc.tensor.matmul(s_row[h % 2][0:Q, 0:KEYS], q_stack[0:ROWS, b.slot, h, :],
                                     k_stack[0:ROWS, b.slot, h, 0:KEYS], start=True, stop=True).then_inc(s_row_done, 1)

                def max_transposed(b, d):
                    pe.wait_ge(max_done, H * b.index + H)
                    if d.valid():
                        pe.wait_ge(z_step, Z_STEPS * (d.index + 1))
                    else:
                        after(pe, m_step, M_STEPS * b.index)
                    nc.tensor.transpose(tr[0:H, 0:Q], negmax[:], ident[0:Q, 0:Q]).then_inc(mt_done, 1)

                def scores(b, g):
                    if g == 0:
                        pe.wait_ge(m_stacked[b.slot], 48 * b.turn + 48)
                    after(pe, exp_done, NG * b.index + g - 1)
                    kt = g % KT
                    n = LAST if kt == KT - 1 else 128
                    for j in range(4):
                        h = 4 * (g // KT) + j
                        last = nc.tensor.matmul(s_t[g % 2][0:n, j * Q:j * Q + Q], k_stack[0:MROWS, b.slot, h, kt * 128:kt * 128 + n],
                                                q_stack[0:MROWS, b.slot, h, :], start=True, stop=True)
                    last.then_inc(s_t_done, 1)

                def values(b, g):
                    if g == 0:
                        pe.wait_ge(v_ready, b.index + 1)
                        after(pe, zt_copied, b.index)
                    pe.wait_ge(p_ready, NG * b.index + g + 1)
                    kt, grp = g % KT, g // KT
                    n = LAST if kt == KT - 1 else 128
                    for j in range(4):
                        last = nc.tensor.matmul(zt[32 * j:32 * j + 32, grp * Q:grp * Q + Q], v_aug[0:n, b.slot, kt * H + 4 * grp + j, :],
                                                p_t[0:n, g % 4, j * Q:j * Q + Q], start=(kt == 0), stop=(kt == KT - 1))
                    last.then_inc(pv_done, 1)

                def z_rows(d, c, f):
                    pe.wait_ge(zt_copied, d.index + 1)
                    if f.valid():
                        pe.wait_ge(logits_ready, f.index + 1)
                    else:
                        pe.wait_ge(m_step, M_STEPS * (c.index + 1))
                    for grp in range(G):
                        last = nc.tensor.transpose(tr[0:Q, grp * 128:grp * 128 + 128], zt_s[:, grp * Q:grp * Q + Q], ident[:])
                    last.then_inc(zrow_done, 1)

                def zf_transposed(f, c, d):
                    pe.wait_ge(zf_ready, f.index + 1)
                    if c.valid():
                        pe.wait_ge(m_step, M_STEPS * (c.index + 1))
                    else:
                        after(pe, z_step, Z_STEPS * min(d.index, B))
                        after(pe, logits_ready, f.index)
                        pe.wait_ge(m_step, M_STEPS * B)
                    for c in range(2):
                        last = nc.tensor.transpose(tr[:, c * Q:c * Q + Q], zf_s[:, f.slot, c * 128:c * 128 + 128], ident[0:Q, 0:Q])
                    last.then_inc(zft_done, 1)

                def router(f):
                    pe.wait_ge(zft_copied, f.index + 1)
                    for c in range(2):
                        last = nc.tensor.matmul(tr[0:Q, 256:256 + E], zft[:, c * Q:c * Q + Q], rw_s[:, c, :], start=(c == 0), stop=(c == 1))
                    last.then_inc(logits_done, 1)

                pe.wait_ge(const_loaded, 16 * N_CONST)
                pe.wait_ge(memsets, 3)

                def iteration(turn, i):
                    a, b, c, d, f = (Batch(turn, i + k) for k in (2, 1, 0, -1, -3))
                    for s in range(NG):
                        n, g = lagging(turn, i, s, SCORES_LAG)
                        if n.valid():
                            scores(n, g)
                        heads = ROW_SLOTS[s] if b.valid() else ()
                        for h in heads:
                            score_rows(b, h)
                        if a.valid():
                            for item in PROJECTIONS.get(s, ()):
                                project(a, item)
                        if d.valid() and s == Z_SLOTS[1]:
                            z_rows(d, c, f)
                        if f.valid() and s == F_SLOTS[0]:
                            zf_transposed(f, c, d)
                        if f.valid() and s == F_SLOTS[2]:
                            router(f)
                        n, g = lagging(turn, i, s, VALUES_LAG)
                        if n.valid():
                            values(n, g)
                        if b.valid() and s == MAX_SLOT:
                            max_transposed(b, d)

                pipeline(pe, iteration)

            @blk.scalar
            def _(act):
                def copy_parts(a, item):
                    if item == 0:
                        act.wait_ge(dt_done, a.index + 1)
                        after(act, q_done, a.index)
                        nc.scalar.activation(dt_s[:, :, :].rearrange("p c k -> p (c k)"), pj[0][:, 0:2 * Q], ACT.Copy).then_inc(dt_copied, 1)
                    elif item == 1:
                        act.wait_ge(q_done, a.index + 1)
                        for t in range(2):
                            nc.scalar.activation(q_part[:, t, 0, :], pj[0][:, t * Q:t * Q + Q], ACT.Identity,
                                                 bias=bq_s[:, t:t + 1]).then_inc(qh_ready, 1)
                    elif item < 4:
                        t = item - 2
                        act.wait_ge(k_done, 2 * a.index + 1 + t)
                        nc.scalar.activation(k_part[:, t, 0, :], pj[t][:, 0:KEYS], ACT.Identity,
                                             bias=bk_s[:, t:t + 1]).then_inc(kh_ready, 1)
                    elif item == 4:
                        act.wait_ge(q_rest_ready, 2 * a.index + 2)
                        nc.scalar.activation(q_part[:, :, 1], q_rest[:], ACT.Copy).then_inc(qm_ready, 1)
                    elif item == 5:
                        act.wait_ge(k_rest_ready, 2 * a.index + 2)
                        nc.scalar.activation(k_part[:, :, 1], k_rest[:], ACT.Copy).then_inc(km_ready, 1)

                def normalised(b, dst, ready):
                    nc.scalar.activation(dst[:], x_all[:, b.index, :], ACT.Identity, bias=nb0[:, bass.ds(b.index, 1)],
                                         scale=rstd0[:, bass.ds(b.index, 1)]).then_inc(ready, 1)

                def apply_norm(b, nth):
                    act.wait_ge(nb_ready, 3 * b.index + nth + 1)
                    dst, src, ready = ((y, u, norm_ready_y), (u, y, u_normalised), (t1, u, norm_ready_t))[nth]
                    nc.scalar.activation(dst[:], src[:], ACT.Identity, bias=nb[:], scale=rstd[:]).then_inc(ready, 1)

                def exponentials(b, g):
                    act.wait_ge(s_t_done, NG * b.index + g + 1)
                    after(act, pv_done, NG * b.index + g - 3)
                    n = LAST if g % KT == KT - 1 else 128
                    nc.scalar.activation(p_t[0:n, g % 4, :], s_t[g % 2][0:n, 0:4 * Q], ACT.Exp).then_inc(exp_done, 1)

                act.wait_ge(const_loaded, 16 * N_CONST)
                act.wait_ge(nb0_ready, 1)

                def iteration(turn, i):
                    a, b, d, e, f = (Batch(turn, i + k) for k in (2, 1, -1, -2, -3))
                    if a.known and i == 2:
                        act.wait_ge(nb0_ready, 4)
                    for s in range(NG):
                        if a.valid() and s == X_SLOTS[0]:
                            normalised(a, drow, d_ready)
                        n, g = lagging(turn, i, s, SCORES_LAG)
                        if n.valid():
                            exponentials(n, g)
                        if d.valid() and s == Z_SLOTS[0]:
                            act.wait_ge(pv_done, NG * d.index + NG)
                            after(act, zrow_done, d.index)
                            nc.scalar.activation(zt_s[:], zt[:, 0:G * Q], ACT.Copy).then_inc(zt_copied, 1)
                        if f.valid() and s == F_SLOTS[1]:
                            act.wait_ge(zft_done, f.index + 1)
                            nc.scalar.activation(zft[:], tr[:, 0:2 * Q], ACT.Copy).then_inc(zft_copied, 1)
                        if a.valid():
                            if s == 0 and b.valid():
                                act.wait_ge(q_stored[b.slot], 16 * b.turn + 16)
                                act.wait_ge(k_stored[b.slot], 16 * b.turn + 16)
                            for item in ACT_ITEMS.get(s, ()):
                                copy_parts(a, item)
                        if d.valid() and s == X_SLOTS[1]:
                            normalised(d, td, td_ready)
                        if e.valid() and s in NORM_SLOTS:
                            apply_norm(e, NORM_SLOTS.index(s))
                        if b.valid() and s == MAX_STEPS[0]:
                            act.wait_ge(mt_done, b.index + 1)
                            p = Batch(turn, i)
                            if p.valid():
                                act.wait_ge(m_stacked[p.slot], 48 * p.turn + 48)
                            nc.scalar.activation(m_part[:, 0], tr[0:H, 0:Q], ACT.Copy).then_inc(m_high_ready, 1)
                        if b.valid() and s == MAX_STEPS[2]:
                            act.wait_ge(m_step, M_STEPS * b.index + 1)
                            nc.scalar.activation(m_part[:, 1], m_rest[:], ACT.Copy).then_inc(m_mid_ready, 1)

                pipeline(act, iteration)

            @blk.vector
            def _(dve):
                v = nc.vector
                v.memset(ct[:, :, :, KEYS:KPAD], 0.0).then_inc(pad_written, 1)
                v.memset(ones_row[:], 1.0).then_inc(ones_written, 1)

                count = [0]

                def step0(ins):
                    count[0] += 1
                    ins.then_inc(ln0_step, 1)
                    dve.wait_ge(ln0_step, count[0])

                def x_statistics(k):
                    dve.wait_ge(x_loaded[k], 16)
                    with dve.Fori(2 * k, 2 * k + 2) as t:
                        for j in range(4):
                            b = t * 4 + j if j else t * 4
                            v.bn_stats(stats0[:, b, :], x_all[:, b, :]).then_inc(stats0_done, 1)
                    dve.wait_ge(stats0_done, 8 * (k + 1))
                    part = slice(8 * k, 8 * k + 8)
                    me, mo = stats0[:, part, 1], stats0[:, part, 4]
                    l0, l1, l2 = (t[:, part] for t in ln0[0:3])
                    step0(v.tensor_tensor(l0, me, mo, ALU.add))
                    step0(v.tensor_scalar(mean0[:, part], l0, 0.5, None, ALU.mult))
                    step0(v.tensor_tensor(l0, me, mo, ALU.subtract))
                    step0(v.tensor_tensor(l1, l0, l0, ALU.mult))
                    step0(v.tensor_tensor(l2, stats0[:, part, 2], stats0[:, part, 5], ALU.add))
                    step0(v.tensor_scalar(l1, l1, 0.25, EPS, ALU.mult, ALU.add))
                    step0(v.tensor_scalar(l2, l2, 1.0 / D, None, ALU.mult))
                    step0(v.tensor_tensor(l0, l2, l1, ALU.add))
                    dve.wait_ge(rstd0_ready, k + 1)
                    v.scalar_tensor_tensor(nb0[:, part], mean0[:, part], -1.0, rstd0[:, part], ALU.mult, ALU.mult).then_inc(nb0_ready, 1)

                x_statistics(0)
                dve.wait_ge(const_loaded, 16 * N_CONST)

                def projections(a, item):
                    if item == 1:
                        for t in range(2):
                            dve.wait_ge(qh_ready, 2 * a.index + 2)
                            after(dve, q_low_ready, a.index)
                            v.scalar_tensor_tensor(q_rest[:, t], pj[0][:, t * Q:t * Q + Q], bq_s[:, t:t + 1], q_part[:, t, 0, :],
                                                   ALU.add, ALU.subtract).then_inc(q_rest_ready, 1)
                    elif item < 4:
                        t = item - 2
                        dve.wait_ge(kh_ready, 2 * a.index + 1 + t)
                        after(dve, k_low_ready, a.index)
                        v.scalar_tensor_tensor(k_rest[:, t], pj[t][:, 0:KEYS], bk_s[:, t:t + 1], k_part[:, t, 0, :],
                                               ALU.add, ALU.subtract).then_inc(k_rest_ready, 1)
                    elif item == 4:
                        dve.wait_ge(v_done, 2 * a.index + 1)
                        bias2 = bv_s[:, :].unsqueeze(1).broadcast_to([128, 2, D])
                        v.tensor_tensor(v_raw[:, 0:2 * H, :].rearrange("p (t h) d -> p t (h d)", t=2), pj[1][:, :].rearrange("p (t n) -> p t n", t=2),
                                        bias2, ALU.add).then_inc(v_biased, 1)
                    elif item == 5:
                        dve.wait_ge(v_done, 2 * a.index + 2)
                        v.tensor_tensor(v_raw[:, 2 * H:3 * H, :].rearrange("p h d -> p (h d)"), pj[0][:, 0:D],
                                        bv_s[:, :], ALU.add).then_inc(v_biased, 1)
                    elif item == 6:
                        dve.wait_ge(v_biased, 2 * a.index + 2)
                        after(dve, v_ready, a.index)
                        v.tensor_scalar(v_neg[:], v_raw[:], 0.0, None, ALU.min).then_inc(v_neg_ready, 1)
                        v.tensor_scalar(v_pos[:], v_raw[:], 0.0, None, ALU.max).then_inc(v_neg_ready, 1)

                def row_max(b, h):
                    dve.wait_ge(s_row_done, H * b.index + h + 1)
                    if h == 0:
                        after(dve, mt_done, b.index)
                    v.tensor_reduce(negmax[:, h:h + 1], s_row[h % 2][0:Q, 0:KEYS], AXIS.X, ALU.max, negate=True).then_inc(max_done, 1)

                def max_rest(b):
                    dve.wait_ge(m_high_ready, b.index + 1)
                    v.tensor_tensor(m_rest[:], tr[0:H, 0:Q], m_part[:, 0], ALU.subtract).then_inc(m_step, 1)

                def max_low(b):
                    dve.wait_ge(m_mid_ready, b.index + 1)
                    v.tensor_tensor(m_part[:, 2], m_rest[:], m_part[:, 1], ALU.subtract).then_inc(m_step, 1)

                def guard(b, g):
                    dve.wait_ge(exp_done, NG * b.index + g + 1)
                    n = LAST if g % KT == KT - 1 else 128
                    v.tensor_scalar(p_t[0:n, g % 4, :], p_t[0:n, g % 4, :], 0.0, None, ALU.max).then_inc(p_ready, 1)

                heads = tr[0:Q, :].rearrange("q (h w) -> q h w", w=32)

                def z_denominator(b):
                    dve.wait_ge(zrow_done, b.index + 1)
                    v.tensor_scalar(den[:], heads[:, :, DH], TINY, None, ALU.max).then_inc(z_step, 1)

                def z_reciprocal(b):
                    dve.wait_ge(z_step, Z_STEPS * b.index + 1)
                    v.reciprocal(rden[:], den[:]).then_inc(z_step, 1)

                def z_normalised(b):
                    dve.wait_ge(z_step, Z_STEPS * b.index + 2)
                    p = Batch(b.turn, b.slot - 1) if not b.known else Batch(0, b.index - 1)
                    if p.valid():
                        dve.wait_ge(z_stored[p.slot], 16 * p.turn + 16)
                    v.tensor_tensor(zn[:], heads[:, :, 0:DH], rden[:].unsqueeze(2).broadcast_to([Q, H, DH]),
                                    ALU.mult).then_inc(z_step, 1)

                def statistics(b, nth):
                    if nth == 0:
                        dve.wait_ge(u_ready, b.index + 1)
                    elif nth == 1:
                        dve.wait_ge(pool_step, POOL_STEPS * b.index + 2)
                    else:
                        dve.wait_ge(u_normalised, b.index + 1)
                    v.bn_stats(st6[:], (u, y, u)[nth][:]).then_inc(tail_step, 1)

                def aggregate(b, nth):
                    dve.wait_ge(tail_step, TAIL * b.index + 2 * nth + 1)
                    v.tensor_copy(var[:], st6[:, 1:2])
                    v.bn_aggr(mv[:], st6[:]).then_inc(tail_step, 1)

                def mean_and_variance(b, nth):
                    dve.wait_ge(tail_step, TAIL * b.index + 2 * nth + 2)
                    v.tensor_scalar(nmean[:], mv[:, 0:1], -1.0, None, ALU.mult).then_inc(norm_ready, 1)
                    v.tensor_scalar(var[:], mv[:, 1:2], EPS, None, ALU.add).then_inc(norm_ready, 1)

                TAIL = 6

                def add_logits(b):
                    dve.wait_ge(logits_done, b.index + 1)
                    v.tensor_tensor(logits[:, b.index, :], tr[0:Q, 256:256 + E], rb_s[:], ALU.add).then_inc(logits_ready, 1)

                def iteration(turn, i):
                    a, b, d, e, f = (Batch(turn, i + k) for k in (2, 1, -1, -2, -3))
                    for s in range(NG):
                        n, g = lagging(turn, i, s, GUARD_LAG)
                        if n.valid():
                            guard(n, g)
                        nth = TAIL_SLOTS.index(s - 1) if e.valid() and s - 1 in TAIL_SLOTS[0:2] else None
                        if nth is not None:
                            aggregate(e, nth)
                        heads_now = ROW_SLOTS[s] if b.valid() else ()
                        for h in heads_now[:1]:
                            row_max(b, h)
                        if nth is not None:
                            mean_and_variance(e, nth)
                        for h in heads_now[1:]:
                            row_max(b, h)
                        if a.valid() and s in DVE_ITEMS:
                            projections(a, DVE_ITEMS[s])
                        if a.valid() and s == V_SLOT:
                            projections(a, 6)
                        if e.valid() and s in TAIL_SLOTS:
                            statistics(e, TAIL_SLOTS.index(s))
                        if f.valid() and s == F_SLOTS[3]:
                            add_logits(f)
                        ends_here = e.valid() and s == TAIL_SLOTS[2]
                        if d.valid() and s == Z_SLOTS[2]:
                            z_denominator(d)
                        if ends_here:
                            aggregate(e, 2)
                        if d.valid() and s == Z_SLOTS[2]:
                            z_reciprocal(d)
                        if ends_here:
                            mean_and_variance(e, 2)
                        if d.valid() and s == Z_SLOTS[2]:
                            z_normalised(d)
                        if b.valid() and s == MAX_STEPS[1]:
                            max_rest(b)
                        if b.valid() and s == MAX_STEPS[3]:
                            max_low(b)
                    for k in X_ROUNDS.get(i, ()) if a.known else ():
                        x_statistics(k)

                pipeline(dve, iteration)

        ffn = ExitStack()
        with ffn:
            w2_s = sb(ffn, "w2_s", [128, 4, E, D])
            b1_s = sb(ffn, "b1_s", [128, E, HF])
            b2_s = sb(ffn, "b2_s", [128, E, D])
            cst = sb(ffn, "cst", [Q, E + B + 128 + 1])
            sums = sb(ffn, "sums", [Q, 2 * Q])
            rev, steps, lanes, query = cst[:, 0:E], cst[:, E:E + B], cst[:, E + B:E + B + 128], cst[:, E + B + 128:]
            pr = sb(ffn, "pr", [Q, B, E])
            big = [sb(ffn, f"big{k}", [Q, B, E]) for k in range(2)]
            choice = sb(ffn, "choice", [Q, 2, B, E])
            cum = [sb(ffn, f"cum{k}", [Q, 16 + B, E]) for k in range(2)]
            col = [sb(ffn, f"col{k}", [Q, B]) for k in range(4)]
            pos = sb(ffn, "pos", [Q, 2, B])
            pos_i = [sb(ffn, f"pos_i{k}", [Q, 2, B], I32) for k in range(3)]
            lane = sb(ffn, "lane", [Q, 2, B])
            tile_of = sb(ffn, "tile_of", [Q, 2, B])
            tile_hot = sb(ffn, "tile_hot", [Q, 2, CH, NT], BF16)
            over = sb(ffn, "over", [Q, E, B])
            ends = [sb(ffn, f"ends{k}", [Q, 4 + E]) for k in range(2)]
            first = sb(ffn, "first", [Q, E])
            past = sb(ffn, "past", [Q, NT, E])
            te = sb(ffn, "te", [Q, NT])
            te_i = sb(ffn, "te_i", [Q, NT], I32)
            lane_hot = sb(ffn, "lane_hot", [Q, 2, CH, 128], BF16)
            picked = sb(ffn, "picked", [Q, 2, CH, 2, NT], BF16)
            slot_c = sb(ffn, "slot_c", [128, NT])
            idx_t = [sb(ffn, f"idx_t{k}", [128, NT]) for k in range(2)]
            idx_g = sb(ffn, "idx_g", [128, 2], U32)
            idx_s = sb(ffn, "idx_s", [128, 2], U32)
            zg = sb(ffn, "zg", [128, 2, D])
            zgt = sb(ffn, "zgt", [128, 2, 2 * 128])
            hid = sb(ffn, "hid", [128, 2, HF])
            hidt = sb(ffn, "hidt", [128, 2, HF])
            ys = sb(ffn, "ys", [128, 2, D])

            p_zt = pb(ffn, "p_zt", [128, 512])
            p_h = [pb(ffn, f"p_h{k}", [128, 512]) for k in range(2)]
            p_ht = [pb(ffn, f"p_ht{k}", [128, 512]) for k in range(2)]
            p_y = [pb(ffn, f"p_y{k}", [128, 512]) for k in range(2)]
            p_r = pb(ffn, "p_r", [128, 512])

            w2_loaded, cst_loaded, x2_stored = sem("w2_loaded"), sem("cst_loaded"), sem("x2_stored")
            route_step, exp_ready, picks_ready, sums_done, picked_done = (sem(k) for k in ("route_step", "exp_ready", "picks_ready", "sums_done", "picked_done"))
            tile_hot_ready, lane_hot_ready, number_ready, query_ready = (sem(k) for k in ("tile_hot_ready", "lane_hot_ready", "number_ready", "query_ready"))
            tiles_known = sem("tiles_known")
            idx_g_ready, idx_s_ready = sem("idx_g_ready"), sem("idx_s_ready")
            gathered = [sem(f"gathered{k}") for k in range(2)]
            scattered = [sem(f"scattered{k}") for k in range(2)]
            zgt_done, zgt_copied, up_done, biased, gelu_done = (sem(k) for k in ("zgt_done", "zgt_copied", "up_done", "biased", "gelu_done"))
            ht_done, ht_copied, down_done, y_ready = (sem(k) for k in ("ht_done", "ht_copied", "down_done", "y_ready"))

            blk = ffn.enter_context(nc.Block())

            @blk.sync
            def _(sp):
                sp.dma_start(cst[:], route_c).then_inc(cst_loaded, 16)
                sp.dma_start(sums[:], sum_c).then_inc(cst_loaded, 16)
                for e in range(E):
                    sp.dma_start(w2_s[:, :, e, :], w2[e].rearrange("(c p) f -> p c f", p=128)).then_inc(w2_loaded, 16)
                sp.dma_start(b1_s[:], b1.unsqueeze(0).broadcast_to([128, E, HF])).then_inc(w2_loaded, 16)
                sp.dma_start(b2_s[:], b2.unsqueeze(0).broadcast_to([128, E, D])).then_inc(w2_loaded, 16)

            N_W2 = 16 * (E + 2)

            def tiles(eng, step):
                for k in range(2):
                    step(Tile(0, k))
                with eng.Fori(1, (NT - 5) // 2) as turn:
                    for r in range(2):
                        step(Tile(turn, r))
                for k in range(NT - 5, NT):
                    step(Tile(0, k))

            @blk.tensor
            def _(pe):
                pe.wait_ge(cst_loaded, 32)
                pe.wait_ge(picks_ready, 1)
                big0 = big[0][:].rearrange("q b e -> q (b e)")
                nc.tensor.matmul(p_r[0:Q, 0:B * E], sums[:, 0:Q], big0, start=True, stop=True)
                nc.tensor.matmul(p_r[0:Q, B * E:2 * B * E], sums[:, Q:2 * Q], big0, start=True, stop=True).then_inc(sums_done, 1)
                for n in range(2 * B):
                    if n % CH == 0:
                        for ready in (lane_hot_ready, number_ready, query_ready):
                            pe.wait_ge(ready, n // CH + 1)
                    last = nc.tensor.matmul(p_y[0][:, 0:2 * NT], lane_hot[:, n // CH % 2, n % CH, :],
                                            picked[:, n // CH % 2, n % CH].rearrange("q a t -> q (a t)"),
                                            start=(n == 0), stop=(n == 2 * B - 1))
                    if n % CH == CH - 1:
                        last.then_inc(picked_done, 1)

                def rows_transposed(k):
                    pe.wait_ge(gathered[k.slot], 16 * k.turn + 16)
                    after(pe, zgt_copied, k.index)
                    for c in range(2):
                        last = nc.tensor.transpose(p_zt[:, c * 128:c * 128 + 128], zg[:, k.slot, c * 128:c * 128 + 128], ident[:])
                    last.then_inc(zgt_done, 1)

                def expert(k):
                    return pe.value_load(te_i[0:1, bass.ds(k.index, 1)], min_val=0, max_val=E - 1)

                def up(k, e):
                    pe.wait_ge(zgt_copied, k.index + 1)
                    after(pe, biased, k.index - 1)
                    for c in range(2):
                        last = nc.tensor.matmul(p_h[k.slot][:], zgt[:, k.slot, c * 128:c * 128 + 128], w1_s[:, c, bass.ds(e, 1), :].rearrange("p e f -> p (e f)"),
                                                start=(c == 0), stop=(c == 1))
                    last.then_inc(up_done, 1)

                def hidden_transposed(k):
                    pe.wait_ge(gelu_done, k.index + 1)
                    after(pe, ht_copied, k.index - 1)
                    for c in range(4):
                        last = nc.tensor.transpose(p_ht[k.slot][:, c * 128:c * 128 + 128], hid[:, k.slot, c * 128:c * 128 + 128], ident[:])
                    last.then_inc(ht_done, 1)

                def down(k):
                    e = pe.value_load(te_i[0:1, bass.ds(k.index, 1)], min_val=0, max_val=E - 1)
                    pe.wait_ge(ht_copied, k.index + 1)
                    after(pe, y_ready, k.index - 1)
                    for c in range(4):
                        last = nc.tensor.matmul(p_y[k.slot][:, 0:D], hidt[:, k.slot, c * 128:c * 128 + 128], w2_s[:, c, bass.ds(e, 1), :].rearrange("p e f -> p (e f)"),
                                                start=(c == 0), stop=(c == 3))
                    last.then_inc(down_done, 1)

                def step(k):
                    more = not k.known or k.index + 1 < NT
                    e = expert(k.later(1)) if more else None
                    if not k.known or k.index + 2 < NT:
                        rows_transposed(k.later(2))
                    if more:
                        up(k.later(1), e)
                    hidden_transposed(k)
                    if not k.known or k.index >= 1:
                        down(k.later(-1))

                pe.wait_ge(tiles_known, 1)
                pe.wait_ge(w2_loaded, N_W2)
                pe.wait_ge(w1_loaded, 16 * E)
                rows_transposed(Tile(0, 0))
                rows_transposed(Tile(0, 1))
                up(Tile(0, 0), expert(Tile(0, 0)))
                tiles(pe, step)
                down(Tile(0, NT - 1))

            @blk.scalar
            def _(act):
                act.wait_ge(route_step, 2)
                nc.scalar.activation(pr[:].rearrange("q b e -> q (b e)"), big[1][:].rearrange("q b e -> q (b e)"), ACT.Exp).then_inc(exp_ready, 1)

                for m in range(2 * B // CH):
                    act.wait_ge(tile_hot_ready, m + 1)
                    nc.scalar.activation(picked[:, m % 2, :, 1, :], tile_hot[:, m % 2], ACT.Copy, scale=query).then_inc(query_ready, 1)

                def up(k):
                    act.wait_ge(zgt_done, k.index + 1)
                    after(act, up_done, k.index - 1)
                    nc.scalar.activation(zgt[:, k.slot], p_zt[:, 0:256], ACT.Copy).then_inc(zgt_copied, 1)

                def gelu(k):
                    act.wait_ge(biased, k.index + 1)
                    nc.scalar.activation(hid[:, k.slot], hid[:, k.slot], ACT.Gelu).then_inc(gelu_done, 1)

                def step(k):
                    if not k.known or k.index + 2 < NT:
                        up(k.later(2))
                    act.wait_ge(ht_done, k.index + 1)
                    after(act, down_done, k.index - 1)
                    nc.scalar.activation(hidt[:, k.slot], p_ht[k.slot][:], ACT.Copy).then_inc(ht_copied, 1)
                    if not k.known or k.index + 1 < NT:
                        gelu(k.later(1))

                up(Tile(0, 0))
                up(Tile(0, 1))
                gelu(Tile(0, 0))
                tiles(act, step)

            @blk.gpsimd
            def _(pool):
                for m in range(2 * B // CH):
                    pool.wait_ge(tile_hot_ready, m + 1)
                    number = lanes[:, m * CH:m * CH + CH].unsqueeze(2).broadcast_to([Q, CH, NT])
                    nc.gpsimd.tensor_tensor(picked[:, m % 2, :, 0, :], tile_hot[:, m % 2], number, ALU.mult).then_inc(number_ready, 1)
                gathers = [pool.alloc_register(f"gathers{k}") for k in range(2)]
                scatters = [pool.alloc_register(f"scatters{k}") for k in range(2)]
                pool.reg_mov(gathers[0], 1)
                pool.reg_mov(scatters[0], 1)
                zf_rows = zf_d.rearrange("b q d -> (b q) d")

                def gather(k):
                    pool.wait_ge(idx_g_ready, k.index + 1 if k.known else gathers[k.slot])
                    pool.reg_add(gathers[1 - k.slot], gathers[k.slot], 1)
                    pool.indirect_dma_start(zg[:, k.slot, :], None, zf_rows, bass.IndirectOffsetOnAxis(idx_g[:, k.slot:k.slot + 1], 0),
                                            bounds_check=B * Q - 1).then_inc(gathered[k.slot], 16)

                gather(Tile(0, 0))
                gather(Tile(0, 1))

                gather(Tile(0, 2))
                gather(Tile(0, 3))

                def step(k):
                    if not k.known or k.index + 4 < NT:
                        gather(k.later(4))
                    if k.known and k.index == 0:
                        return
                    k = k.later(-1)
                    pool.wait_ge(y_ready, k.index + 1 if k.known else scatters[k.slot])
                    pool.reg_add(scatters[1 - k.slot], scatters[k.slot], 1)
                    pool.indirect_dma_start(y_d, bass.IndirectOffsetOnAxis(idx_s[:, k.slot:k.slot + 1], 0), ys[:, k.slot, :], None,
                                            bounds_check=2 * B * Q - 1, oob_is_err=False).then_inc(scattered[k.slot], 16)

                tiles(pool, step)
                step(Tile(0, NT))
                for s in range(2):
                    pool.wait_ge(scattered[s], 16 * len(range(s, NT, 2)))

            @blk.vector
            def _(dve):
                v = nc.vector
                n = [0]

                def step(ins):
                    n[0] += 1
                    ins.then_inc(route_step, 1)
                    dve.wait_ge(route_step, n[0])

                def over_e(t):
                    return t.unsqueeze(2).broadcast_to([Q, B, E])

                revb = rev.unsqueeze(1).broadcast_to([Q, B, E])
                step(v.tensor_reduce(col[0][:], logits[:], AXIS.X, ALU.max))
                step(v.tensor_tensor(big[1][:], logits[:], over_e(col[0][:]), ALU.subtract))
                dve.wait_ge(exp_ready, 1)
                dve.wait_ge(cst_loaded, 32)
                step(v.tensor_reduce(col[0][:], pr[:], AXIS.X, ALU.add))
                step(v.reciprocal(col[1][:], col[0][:]))
                step(v.tensor_tensor(pr[:], pr[:], over_e(col[1][:]), ALU.mult))
                step(v.tensor_copy(big[0][:], pr[:]))
                for c in range(2):
                    step(v.tensor_reduce(wt[:, c], big[0][:], AXIS.X, ALU.max))
                    step(v.tensor_tensor(big[1][:], big[0][:], over_e(wt[:, c]), ALU.is_equal))
                    step(v.tensor_tensor(big[1][:], big[1][:], revb, ALU.mult))
                    step(v.tensor_reduce(col[c][:], big[1][:], AXIS.X, ALU.max))
                    step(v.tensor_tensor(choice[:, c], revb, over_e(col[c][:]), ALU.is_equal))
                    if c == 0:
                        step(v.scalar_tensor_tensor(big[0][:], choice[:, 0], -2.0, pr[:], ALU.mult, ALU.add))
                step(v.tensor_tensor(big[0][:], choice[:, 0], choice[:, 1], ALU.add))
                v.tensor_copy(col[3][:], wt[:, 0]).then_inc(picks_ready, 1)
                step(v.tensor_tensor(col[0][:], wt[:, 0], wt[:, 1], ALU.add))
                step(v.tensor_scalar(col[0][:], col[0][:], 1e-8, None, ALU.max))
                step(v.reciprocal(col[1][:], col[0][:]))
                for c in range(2):
                    step(v.tensor_tensor(wt[:, c], wt[:, c], col[1][:], ALU.mult))
                dve.wait_ge(sums_done, 1)
                for k in range(2):
                    step(v.memset(cum[k][:, 0:16, :], 0.0))
                    step(v.memset(ends[k][:, 0:4], 0.0))
                step(v.tensor_copy(cum[0][:, 16:, :].rearrange("q b e -> q (b e)"), p_r[0:Q, B * E:2 * B * E]))
                at = 0
                for k in (1, 2, 4, 8, 16):
                    step(v.tensor_tensor(cum[1 - at][:, 16:, :], cum[at][:, 16:, :], cum[at][:, 16 - k:16 + B - k, :], ALU.add))
                    at = 1 - at
                count = cum[at][:, 15 + B, :]
                step(v.tensor_tensor(over[:], count.unsqueeze(2).broadcast_to([Q, E, B]), steps.unsqueeze(1).broadcast_to([Q, E, B]), ALU.is_gt))
                step(v.tensor_reduce(ends[0][:, 4:], over[:], AXIS.X, ALU.add))
                en = 0
                for k in (1, 2, 4):
                    step(v.tensor_tensor(ends[1 - en][:, 4:], ends[en][:, 4:], ends[en][:, 4 - k:4 + E - k], ALU.add))
                    en = 1 - en
                step(v.tensor_scalar(first[:], ends[en][:, 3:3 + E], 128.0, None, ALU.mult))
                step(v.tensor_tensor(past[:], lanes[:, 0:NT].unsqueeze(2).broadcast_to([Q, NT, E]),
                                     ends[en][:, 4:].unsqueeze(1).broadcast_to([Q, NT, E]), ALU.is_ge))
                step(v.tensor_reduce(te[:], past[:], AXIS.X, ALU.add))
                step(v.tensor_scalar(te_i[:], te[:], float(E - 1), None, ALU.min))
                step(v.tensor_tensor(big[1][:], cum[at][:, 15:15 + B, :], first[:].unsqueeze(1).broadcast_to([Q, B, E]), ALU.add))
                step(v.tensor_tensor(big[1][:].rearrange("q b e -> q (b e)"), p_r[0:Q, 0:B * E], big[1][:].rearrange("q b e -> q (b e)"), ALU.add))
                for c in range(2):
                    step(v.tensor_tensor(pr[:], big[1][:], choice[:, c], ALU.mult))
                    step(v.tensor_reduce(pos[:, c], pr[:], AXIS.X, ALU.add))
                step(v.tensor_copy(pos_i[0][:], pos[:]))
                step(v.tensor_scalar(pos_i[1][:], pos_i[0][:], 7, None, ALU.logical_shift_right))
                step(v.tensor_scalar(pos_i[2][:], pos_i[0][:], 127, None, ALU.bitwise_and))
                step(v.tensor_copy(tile_of[:], pos_i[1][:]))
                step(v.tensor_copy(lane[:], pos_i[2][:]))
                for m in range(2 * B // CH):
                    c, b0, h = m * CH // B, m * CH % B, m % 2

                    def part(t, w):
                        return t[:, c, b0:b0 + CH].unsqueeze(2).broadcast_to([Q, CH, w])

                    if m >= 2:
                        dve.wait_ge(picked_done, m - 1)
                    v.tensor_tensor(tile_hot[:, h], lanes[:, 0:NT].unsqueeze(1).broadcast_to([Q, CH, NT]), part(tile_of, NT), ALU.is_equal).then_inc(tile_hot_ready, 1)
                    v.tensor_tensor(lane_hot[:, h], lanes.unsqueeze(1).broadcast_to([Q, CH, 128]), part(lane, 128), ALU.is_equal).then_inc(lane_hot_ready, 1)
                dve.wait_ge(picked_done, 2 * B // CH)
                step(v.tensor_copy(idx_t[0][:], p_y[0][:, 0:NT]))
                step(v.scalar_tensor_tensor(slot_c[:], idx_t[0][:], float(Q), p_y[0][:, NT:2 * NT], ALU.mult, ALU.add))
                cd = slot_c[:]
                step(v.tensor_scalar(idx_t[0][:], cd, float(B * Q), -float(B * Q), ALU.is_gt, ALU.mult))
                step(v.tensor_tensor(idx_t[0][:], idx_t[0][:], cd, ALU.add))
                step(v.tensor_scalar(idx_t[0][:], idx_t[0][:], -1.0, 0.0, ALU.add, ALU.max))
                step(v.tensor_scalar(idx_t[1][:], cd, 0.0, float(4 * B * Q), ALU.is_equal, ALU.mult))
                step(v.tensor_tensor(idx_t[1][:], idx_t[1][:], cd, ALU.add))
                step(v.tensor_scalar(idx_t[1][:], idx_t[1][:], -1.0, None, ALU.add))
                v.tensor_copy(past[:, 0, :], past[:, 1, :]).then_inc(tiles_known, 1)

                def to_gather(k):
                    v.tensor_scalar(idx_g[:, k.slot:k.slot + 1], idx_t[0][:, bass.ds(k.index, 1)], 0.0, None, ALU.add).then_inc(idx_g_ready, 1)

                def bias(k):
                    e = dve.value_load(te_i[0:1, bass.ds(k.index, 1)], min_val=0, max_val=E - 1)
                    dve.wait_ge(up_done, k.index + 1)
                    after(dve, ht_done, k.index - 1)
                    v.tensor_tensor(hid[:, k.slot], p_h[k.slot][:], b1_s[:, bass.ds(e, 1), :].rearrange("p e f -> p (e f)"), ALU.add).then_inc(biased, 1)

                def result(k):
                    e = dve.value_load(te_i[0:1, bass.ds(k.index, 1)], min_val=0, max_val=E - 1)
                    after(dve, scattered[k.slot], 16 * k.turn)
                    v.tensor_scalar(idx_s[:, k.slot:k.slot + 1], idx_t[1][:, bass.ds(k.index, 1)], 0.0, None, ALU.add).then_inc(idx_s_ready, 1)
                    dve.wait_ge(down_done, k.index + 1)
                    dve.wait_ge(idx_s_ready, k.index + 1)
                    v.tensor_tensor(ys[:, k.slot], p_y[k.slot][:, 0:D], b2_s[:, bass.ds(e, 1), :].rearrange("p e f -> p (e f)"), ALU.add).then_inc(y_ready, 1)

                def tile_step(k):
                    if not k.known or k.index + 1 < NT:
                        bias(k.later(1))
                    if not k.known or k.index >= 1:
                        result(k.later(-1))
                    if not k.known or k.index + 4 < NT:
                        dve.wait_ge(zgt_done, k.index + 3)
                        to_gather(k.later(4))

                dve.wait_ge(w2_loaded, N_W2)
                to_gather(Tile(0, 0))
                to_gather(Tile(0, 1))
                for k in (2, 3):
                    dve.wait_ge(zgt_done, k - 1)
                    to_gather(Tile(0, k))
                bias(Tile(0, 0))
                tiles(dve, tile_step)
                result(Tile(0, NT - 1))

        end = ExitStack()
        with end:
            PARTS = 8
            W = B // PARTS
            y1 = [[sb(end, f"y{c}_{k}", [Q, W, D]) for k in range(PARTS)] for c in range(2)]
            y_loaded = [sem(f"y_loaded{k}") for k in range(PARTS)]
            sum_step = sem("sum_step")
            blk = end.enter_context(nc.Block())
            yv = y_d.rearrange("(c b q) d -> c q b d", c=2, q=Q)
            ov = out.rearrange("b q d -> q b d")

            @blk.sync
            def _(sp):
                for m in range(PARTS):
                    for c in range(2):
                        sp.dma_start(y1[c][m][:], yv[c, :, m * W:m * W + W]).then_inc(y_loaded[m], 16)

            @blk.scalar
            def _(act):
                for m in range(PARTS):
                    act.wait_ge(sum_step, 2 * W * (m + 1))
                    act.dma_start(ov[:, m * W:m * W + W], x_all[:, m * W:m * W + W]).then_inc(out_stored, 16)
                act.wait_ge(out_stored, 16 * PARTS)

            @blk.vector
            def _(dve):
                for m in range(PARTS):
                    dve.wait_ge(y_loaded[m], 32)
                    for c in range(2):
                        for j in range(W):
                            xb = x_all[:, m * W + j, :]
                            nc.vector.scalar_tensor_tensor(xb, y1[c][m][:, j, :], wt[:, c, m * W + j:m * W + j + 1], xb, ALU.mult, ALU.add).then_inc(sum_step, 1)
                        dve.wait_ge(sum_step, W * (2 * m + c + 1))


TAIL_SLOTS = (2, 6, 9)
NORM_SLOTS = (4, 8, 11)
V_SLOT = 10
X_ROUNDS = {-2: (1, 2, 3)}
MAX_SLOT = 10
MAX_STEPS = (10, 10, 10, 11)
Z_SLOTS = (6, 8, 9)
F_SLOTS = (3, 4, 5, 6)
X_SLOTS = (0, 8)
PROJECTIONS = {0: (0, 1), 1: (2, 3), 2: (4,), 3: (5,), 4: (6,), 6: (7,), 7: (8,), 8: (9,)}
ACT_ITEMS = {0: (2,), 1: (3, 0), 2: (5,), 4: (1,), 6: (4,)}
DVE_ITEMS = {1: 2, 2: 3, 5: 1, 8: 4, 9: 5}
ROW_COUNTS = (0, 2, 2, 2, 2, 2, 2, 2, 2, 0, 0, 0)


def kernel(**inputs):
    import numpy as np
    import concourse.bacc as bacc
    from concourse.bass_utils import run_bass_kernel_spmd

    def lay(w):
        return np.ascontiguousarray(np.asarray(w).T.reshape(2, 128, D).transpose(1, 0, 2))

    order = np.arange(D).reshape(2, 8, DH).transpose(0, 2, 1).reshape(-1)

    p = {k.replace("L0_", ""): np.asarray(v) for k, v in inputs.items()}
    ctx = p["ctx_1024"]
    arrays = {
        "x": p["x"],
        "ctx_t": np.ascontiguousarray(ctx.transpose(0, 2, 1).reshape(B, 2, 128, KEYS).transpose(0, 2, 1, 3)),
        "wq_t": lay(p["xattn_Wq"][order]), "bq": p["xattn_bq"][order].reshape(2, 128).T,
        "wk_t": lay(p["xattn_Wk"][order]), "bk": p["xattn_bk"][order].reshape(2, 128).T,
        "wv_t": lay(p["xattn_Wv"]), "bv": p["xattn_bv"],
        "gamma": p["xattn_gamma"], "beta": p["xattn_beta"],
        "ln_g": p["ffn_ln_g"], "ln_b": p["ffn_ln_b"], "rw": p["ffn_rW"], "rb": p["ffn_rb"],
        "w1": p["ffn_W1"], "b1": p["ffn_b1"], "w2": p["ffn_W2"], "b2": p["ffn_b2"],
        "ident_d": np.eye(128, dtype=np.float32),
        "route_c": np.concatenate([np.tile(np.concatenate([np.arange(E, 0, -1), 128 * np.arange(B), np.arange(128)]), (Q, 1)),
                                   1 + np.arange(Q)[:, None]], 1).astype(np.float32),
        "sum_c": np.concatenate([np.triu(np.ones((Q, Q)), 1), np.ones((Q, Q))], 1).astype(np.float32),
    }
    nc = bacc.Bacc("TRN2", target_bir_lowering=False, num_devices=1)
    args = {k: nc.dram_tensor("in_" + k, a.shape, mybir.dt.from_np(a.dtype), kind="ExternalInput").ap() for k, a in arrays.items()}
    args["kscr"] = nc.dram_tensor("kscr", [3, 2, 3, DH, 8, KEYS], BF16, kind="Internal").ap()
    args["qscr"] = nc.dram_tensor("qscr", [3, 2, 3, DH, 8, Q], BF16, kind="Internal").ap()
    args["zscr"] = nc.dram_tensor("zscr", [3, H, Q, DH], FP32, kind="Internal").ap()
    args["zf_d"] = nc.dram_tensor("zf_d", [B, Q, D], FP32, kind="Internal").ap()
    args["y_d"] = nc.dram_tensor("y_d", [2 * B * Q, D], FP32, kind="Internal").ap()
    args["out"] = nc.dram_tensor("out_x", [B, Q, D], FP32, kind="ExternalOutput").ap()
    build(nc, **args)
    r = run_bass_kernel_spmd(nc, [{"in_" + k: np.ascontiguousarray(a) for k, a in arrays.items()}], core_ids=[0])
    return r.results[0]["out_x"]
```
